# Optimizing a Trainium2 kernel written in Bass

```python
import numpy as np
import jax
import jax.numpy as jnp

def _softmax(x, axis=-1):
    return jax.nn.softmax(x, axis=axis)

def _gelu(x):
    return jax.nn.gelu(x, approximate=True)

def _silu(x):
    return jax.nn.silu(x)

def _sigmoid(x):
    return jax.nn.sigmoid(x)

def _layernorm(x, axis=-1, eps=1e-05):
    m = jnp.mean(x, axis=axis, keepdims=True)
    v = jnp.var(x, axis=axis, keepdims=True)
    return (x - m) / jnp.sqrt(v + eps)

def _scatter_add(tgt, idx, src, axis=0):
    return tgt.at[idx].add(src)

def _segment_sum(src, seg, n):
    return jax.ops.segment_sum(src, seg, n)
kernel_name = 'mk_seq_postln_d1_jaxref_r8_8682ca'

def setup_inputs(seed: int=0):
    np.random.seed(seed)
    _w = jnp.asarray

    def _L0_attn_setup():
        import jax, jax.numpy as jnp
        import numpy as np
        import math
        B, T, E = (1, 256, 128)
        H = 16
        D = E // H
        L = 64
        key = jax.random.key(seed)
        ks = jax.random.split(key, 7)
        s = lambda fan: 1.0 / math.sqrt(fan)
        return {'hidden_states': jax.random.normal(ks[0], (B, T, E), dtype=jnp.float32), 'Wq': jax.random.normal(ks[1], (E, E), dtype=jnp.float32) * s(E), 'Wk_down': jax.random.normal(ks[2], (L, E), dtype=jnp.float32) * s(E), 'Wv_down': jax.random.normal(ks[3], (L, E), dtype=jnp.float32) * s(E), 'q_to_latent': jax.random.normal(ks[4], (H, D, L), dtype=jnp.float32) * s(D), 'v_up': jax.random.normal(ks[5], (H, L, D), dtype=jnp.float32) * s(L), 'Wout': jax.random.normal(ks[6], (E, E), dtype=jnp.float32) * s(E)}
    _L0_attn_in = _L0_attn_setup()

    def _L0_ffn_setup():
        import jax, jax.numpy as jnp
        import numpy as np
        B, S, D = (4, 256, 128)
        E, H, TOP_K = (8, 256, 2)
        key = jax.random.key(seed)
        k_x, k_g, k_w1, k_w2, k_w3 = jax.random.split(key, 5)
        s_d = 1.0 / np.sqrt(D)
        s_h = 1.0 / np.sqrt(H)
        return {'x': jax.random.normal(k_x, (B, S, D), dtype=jnp.float32), 'w_gate': jax.random.normal(k_g, (D, E), dtype=jnp.float32) * s_d, 'w1': jax.random.normal(k_w1, (E, D, H), dtype=jnp.float32) * s_d, 'w3': jax.random.normal(k_w3, (E, D, H), dtype=jnp.float32) * s_d, 'w2': jax.random.normal(k_w2, (E, H, D), dtype=jnp.float32) * s_h}
    _L0_ffn_in = _L0_ffn_setup()
    _d = {'L0_attn_hidden_states': _L0_attn_in['hidden_states'], 'L0_attn_Wq': _L0_attn_in['Wq'], 'L0_attn_Wk_down': _L0_attn_in['Wk_down'], 'L0_attn_Wv_down': _L0_attn_in['Wv_down'], 'L0_attn_q_to_latent': _L0_attn_in['q_to_latent'], 'L0_attn_v_up': _L0_attn_in['v_up'], 'L0_attn_Wout': _L0_attn_in['Wout'], 'L0_ffn_w_gate': _L0_ffn_in['w_gate'], 'L0_ffn_w1': _L0_ffn_in['w1'], 'L0_ffn_w3': _L0_ffn_in['w3'], 'L0_ffn_w2': _L0_ffn_in['w2']}
    _x0 = _d['L0_attn_hidden_states']
    _d['L0_attn_hidden_states'] = jax.random.normal(jax.random.fold_in(jax.random.key(seed), 1), (16, 512, 128), dtype=_x0.dtype)
    del _x0
    return _d

def reference(L0_attn_hidden_states, L0_attn_Wq, L0_attn_Wk_down, L0_attn_Wv_down, L0_attn_q_to_latent, L0_attn_v_up, L0_attn_Wout, L0_ffn_w_gate, L0_ffn_w1, L0_ffn_w3, L0_ffn_w2):

    def _L0_attn_ref(hidden_states, Wq, Wk_down, Wv_down, q_to_latent, v_up, Wout):
        import jax, jax.numpy as jnp
        import numpy as np
        import math
        B, T, E = (1, 256, 128)
        H = 16
        D = E // H
        L = 64
        'RA_MLA_Attention forward (default config: coupling_scale=0 so the RA\n            reciprocal-band branch is inactive; no cache, no RoPE, dropout=0).'
        b, t, e = hidden_states.shape
        h, d, l = q_to_latent.shape
        Q = (hidden_states @ Wq.T).reshape(b, t, h, d)
        latent_k = hidden_states @ Wk_down.T
        latent_v = hidden_states @ Wv_down.T
        q_lat = jnp.einsum('bthd,hdl->bthl', Q, q_to_latent)
        logits = jnp.einsum('bthl,bsl->bhts', q_lat, latent_k) / math.sqrt(l)
        causal = jnp.tril(jnp.ones((t, t), dtype=bool))
        logits = jnp.where(causal[None, None], logits, jnp.float32(-1e+30))
        attn = jax.nn.softmax(logits, axis=-1)
        ctx_lat = jnp.einsum('bhts,bsl->bhtl', attn, latent_v)
        heads = jnp.einsum('bhtl,hld->bthd', ctx_lat, v_up)
        out = heads.reshape(b, t, h * d) @ Wout.T
        return out

    def _L0_ffn_ref(x, w_gate, w1, w3, w2):
        import jax, jax.numpy as jnp
        import numpy as np
        B, S, D = (4, 256, 128)
        E, H, TOP_K = (8, 256, 2)
        bsz, seq_len, embed_dim = x.shape
        xt = x.reshape(-1, embed_dim)
        T = xt.shape[0]
        logits = xt @ w_gate
        top_logits, sel = jax.lax.top_k(logits, TOP_K)
        probs = jax.nn.softmax(top_logits, axis=-1).astype(x.dtype)
        h = jax.nn.silu(jnp.einsum('td,edh->eth', xt, w1)) * jnp.einsum('td,edh->eth', xt, w3)
        y = jnp.einsum('eth,ehd->etd', h, w2)
        t_idx = jnp.arange(T)
        yk = y[sel.T, t_idx[None, :], :]
        out = jnp.einsum('ktd,tk->td', yk, probs)
        return out.reshape(bsz, seq_len, embed_dim)
    x = L0_attn_hidden_states
    x = _layernorm(x + _L0_attn_ref(x, L0_attn_Wq, L0_attn_Wk_down, L0_attn_Wv_down, L0_attn_q_to_latent, L0_attn_v_up, L0_attn_Wout), axis=-1)
    x = _layernorm(x + _L0_ffn_ref(x, L0_ffn_w_gate, L0_ffn_w1, L0_ffn_w3, L0_ffn_w2), axis=-1)
    return x

_drawn_inputs = setup_inputs


def setup_inputs(seed=0):
    import zlib

    import numpy as np

    out = dict(_drawn_inputs(seed))
    spreads = {}
    factors = {}
    for name, (base, spread) in spreads.items():
        noise = np.random.default_rng([zlib.crc32(name.encode()), seed]).standard_normal(out[name].shape)
        drawn = base * np.exp(spread * noise) if base else spread * noise
        out[name] = jnp.asarray(drawn.astype(out[name].dtype))
    for name, factor in factors.items():
        out[name] = (out[name] * factor).astype(out[name].dtype)
    return out
```

```python
import concourse.bass as bass
from concourse import mybir
from contextlib import ExitStack

FP32 = mybir.dt.float32
BF16 = mybir.dt.bfloat16
INT32 = mybir.dt.int32
UINT32 = mybir.dt.uint32
ALU = mybir.AluOpType
ACT = mybir.ActivationFunctionType
AX = mybir.AxisListType

P = 128
NEG = -1e30
EPS = 1e-5
PARTS = 3
Q_ROWS = [(0, 0, 3), (3, 1, 2), (5, 2, 1)]
K_ROWS = [(0, 0, 3), (3, 0, 2), (5, 0, 1)]
SLOTS = 6
MAX_ROW = 96
STACK = 3


class Batch:

    def __init__(self, turns, off, count):
        self.turns, self.off, self.count = turns, off, count
        self.num = turns * STACK + off
        self.buf = off % STACK
        self.round = turns + off // STACK

    def plus(self, k):
        return Batch(self.turns, self.off + k, self.count)

    @property
    def exists(self):
        return not isinstance(self.num, int) or 0 <= self.num < self.count


def wait(eng, sem, value):
    if not isinstance(value, int) or value > 0:
        eng.wait_ge(sem, value)


def wait_apart(eng, sem, value, passed):
    if not isinstance(value, int):
        eng.wait_ge(sem, value)
        eng.sem_inc(passed, 1)
    elif value > 0:
        eng.wait_ge(sem, value)


def over_batches(eng, count, step):
    full_from, full_to = 3, count - 2
    turns = (full_to - full_from) // STACK
    for b in range(-2, full_from):
        step(Batch(0, b, count))
    if turns:
        with eng.Fori(0, turns) as i:
            for u in range(STACK):
                step(Batch(i, full_from + u, count))
    for b in range(full_from + turns * STACK, count + 2):
        step(Batch(0, b, count))


def build(nc, hidden, Wq, Wk_down, Wv_down, q_to_latent, v_up, Wout, w_gate, w1, w3, w2, out):
    B, T, E = hidden.shape
    H, D, L = q_to_latent.shape
    TT = T // P
    QUAD = 4
    QUADS = H // QUAD
    HP = QUAD // 2
    EB = 10
    MB = EB // 2
    CT = 32
    SC = float(L) ** -0.5
    X = w_gate.shape[1]
    TOP = 2
    F = w1.shape[2]
    FC = F // P
    TOKENS = B * T
    REGION = TOKENS + P
    ROW = E + 2
    SPARE = X * REGION
    JOBS = -(-(TOP * TOKENS + X * (P - 1)) // P)
    JOBS += JOBS % 2
    NOWHERE = float(4 * TOKENS)

    xs_dram = nc.dram_tensor("expert_rows", (SPARE + P, ROW), FP32, kind="Internal").ap()
    y_dram = nc.dram_tensor("expert_results", (TOP * TOKENS, E), FP32, kind="Internal").ap()
    x1_dram = nc.dram_tensor("x1", (TOKENS, E), FP32, kind="Internal").ap()

    keep = ExitStack()
    base = keep.enter_context(nc.sbuf_tensor("next_row", [P, X], FP32))
    ident = keep.enter_context(nc.sbuf_tensor("ident", [P, P], FP32))
    eps_col = keep.enter_context(nc.sbuf_tensor("eps_col", [P, 1], FP32))
    region0 = keep.enter_context(nc.sbuf_tensor("region0", [P, X], FP32))

    ctx = ExitStack()
    with ctx:
        def sb(name, shape, dt=FP32):
            return ctx.enter_context(nc.sbuf_tensor(name, shape, dt))

        def ps(name, shape, dt=FP32):
            return ctx.enter_context(nc.psum_tensor(name, shape, dt))

        def sem(name):
            return ctx.enter_context(nc.semaphore(name))

        def sems(name, n):
            return [sem(f"{name}{i}") for i in range(n)]

        def dram(name, shape, dt=FP32):
            return nc.dram_tensor(name, shape, dt, kind="Internal").ap()

        parts_dram = [[dram(f"parts_{w}{i}", (PARTS, D, H, T), BF16) for i in range(STACK)] for w in "qk"]
        heads_dram = [dram(f"heads_{i}", (H, D + 1, T)) for i in range(STACK)]
        recip_dram = [dram(f"recip_{i}", (H, T)) for i in range(STACK)]

        ident_bf = sb("ident_bf", [P, P], BF16)
        ahead = sb("ahead", [P, 2, P], BF16)
        wq_nat = sb("wq_nat", [P, E])
        wout_nat = sb("wout_nat", [P, E])
        qtl_nat = sb("qtl_nat", [P, L])
        wkd = sb("wkd", [L, E])
        wvd = sb("wvd", [L, E])
        vup = sb("vup", [L, H, D])
        qtlT = sb("qtlT", [L, P])
        wqT = sb("wqT", [P, H * D])
        wkT = sb("wkT", [P, H * D])
        wvT = sb("wvT", [P, H * D])
        woutT = sb("woutT", [P, E])
        x_in = sb("x_in", [P, STACK, TT, E])
        x_res = sb("x_res", [P, STACK, TT, E])
        xT = sb("xT", [P, T])
        qk_parts = [sb("q_parts", [P, PARTS, T], BF16), sb("k_parts", [P, PARTS, T], BF16)]
        qk_rest = [sb("q_rest", [P, T]), sb("k_rest", [P, T])]
        q_stack = [sb(f"q_stack{i}", [P, H, T], BF16) for i in range(STACK)]
        k_stack = [sb(f"k_stack{i}", [P, H, T], BF16) for i in range(STACK)]
        v_aug = sb("v_aug", [P, STACK, TT * H * 2 * D + CT - 2 * D])
        part_max = sb("part_max", [P, QUADS * HP, 5, 4])
        row_max = sb("row_max", [P, H, TT])
        max_parts = sb("max_parts", [H * TT, PARTS, P], BF16)
        max_rest = sb("max_rest", [H * TT, P])
        probs = sb("probs", [P, 2, EB, T])
        heads_out = sb("heads_out", [P, QUADS, T])
        numer = sb("numer", [P, T])
        denom = sb("denom", [P, T * H // P])
        rden = sb("rden", [P, T * H // P])
        rden_all = sb("rden_all", [P, T])
        headsT = sb("headsT", [P, T])
        resid = sb("resid", [P, TT, E])
        stats = sb("stats", [P, TT, 6])
        mean_var = sb("mean_var", [P, TT, 2])
        log_var = sb("log_var", [P, TT])
        rstd = sb("rstd", [P, TT])
        image = sb("image", [P, TT, TOP, ROW])
        x1T = sb("x1T", [E, T])
        wg = sb("wg", [E, X])
        before = sb("before", [P, P], BF16)
        ones_bf = sb("ones_bf", [P, P], BF16)
        tmp_f = sb("tmp_f", [P, P])
        iota_i = sb("iota_i", [P, X], INT32)
        iota_x = sb("iota_x", [P, X])
        dest_i = sb("dest_i", [P, TT * TOP], INT32)
        dest = sb("dest", [P, TT, TOP])
        logits = sb("logits", [P, TT, X])
        top = sb("top", [P, TT, 8])
        top_at = sb("top_at", [P, TT, 8], UINT32)
        top_f = sb("top_f", [P, TT, TOP])
        chosen_bf = sb("chosen_bf", [P, TT, TOP, X], BF16)
        gap = sb("gap", [P, TT])
        odds = sb("odds", [P, TT])
        odds1 = sb("odds1", [P, TT])
        row_of = sb("row_of", [P, TT, X])
        picked = sb("picked", [P, TT, TOP, X])
        row_f = sb("row_f", [P, TT, TOP])
        row_i = sb("row_i", [P, TT, TOP], UINT32)

        score = ps("score", [P, 2, T])
        maxs = ps("maxs", [P, 2, 2, T])
        attn = ps("attn", [P, T])
        misc = ps("misc", [P, T])

        s_passed_pool, s_passed_dve, s_passed_pe = sem("pool_passed"), sem("dve_passed"), sem("pe_passed")
        s_w = sem("weights_loaded")
        s_const = sem("constants_made")
        s_wt = sem("weight_product_done")
        s_wc = sem("weight_copied")
        s_zero = sems("stacks_cleared", STACK)
        s_vones = sem("v_ones_made")
        s_xin = sems("x_in_loaded", STACK)
        s_xres = sems("x_res_loaded", STACK)
        s_xt = sem("x_transposed")
        s_xtc = sem("xT_copied")
        s_proj = sem("q_or_k_projected")
        s_hi = sem("part0_made")
        s_mid = sem("part1_made")
        s_rest = sem("rest_made")
        s_parts = sem("parts_made")
        s_pst = [sems("q_parts_stored", STACK), sems("k_parts_stored", STACK)]
        s_stk = sems("stack_loaded", STACK)
        s_v = sem("v_projected")
        s_vc = sem("v_copied")
        s_msc = sem("scores_for_max_ready")
        s_mx = sem("block_maxima_taken")
        s_rm = sem("row_max_combined")
        s_nmt = sem("row_max_transposed")
        s_nm0 = sem("max_part0_made")
        s_nmr = sem("max_rest_made")
        s_nm1 = sem("max_part1_made")
        s_nmp = sem("max_parts_made")
        s_nmd = sems("max_rows_loaded", STACK)
        s_sc = sem("scores_ready")
        s_exp = sem("exp_done")
        s_tri = sem("future_cleared")
        s_pv = sem("quad_attended")
        s_oc = sem("quad_copied")
        s_hd = sems("heads_stored", STACK)
        s_nd = sems("numer_denom_loaded", STACK)
        s_rd = sem("recip_made")
        s_rst = sems("recip_stored", STACK)
        s_rl = sems("recip_loaded", STACK)
        s_ht = sem("heads_normalized")
        s_op = sem("out_projected")
        s_res = sem("residual_added")
        s_st = sem("stats_step")
        s_ln = sem("log_made")
        s_rs = sem("rstd_made")
        s_x1 = sem("x1_made")
        s_out = sem("x1_stored")
        s_x1t = sem("x1_transposed")
        s_x1tc = sem("x1T_copied")
        s_lg = sem("logits_ready")
        s_ch = sem("choice_step")
        s_oh = sem("choice_made")
        s_gap = sem("gap_made")
        s_odds = sem("odds_made")
        s_rk = sem("ranks_ready")
        s_rr = sem("ranks_read")
        s_ro = sem("row_step")
        s_im = sem("image_doubled")
        s_rows = sem("rows_made")
        s_sct = sem("rows_scattered")

        WEIGHTS = 8 * 16
        def exps(b, g, k):
            return (b.num * QUADS + g) * EB + k + 1
        def maxes(b, g, k):
            return (b.num * QUADS + g) * MB + k + 1
        TRI = 6
        def quad(b, g):
            return b.num * QUADS + g
        NX = STACK

        x_dram = hidden.rearrange("b (i p) e -> b p i e", p=P)
        x1_v = x1_dram.rearrange("(b i p) e -> b p i e", p=P, i=TT)


        def clear_stacks(eng, i):
            for n, stack in enumerate((q_stack[i], k_stack[i])):
                eng.memset(stack[:].rearrange("p h t -> p (h t)").bitcast(FP32), 0.0).then_inc(s_zero[i], 1)
            eng.wait_ge(s_zero[i], 2)
            eng.memset(k_stack[i][MAX_ROW:P], 1.0).then_inc(s_zero[i], 1)
            eng.wait_ge(s_zero[i], 3)

        block = ctx.enter_context(nc.Block())

        @block.sync
        def _(sp):
            sp.dma_start(wq_nat[:], Wq).then_inc(s_w, 16)
            sp.dma_start(wout_nat[:], Wout).then_inc(s_w, 16)
            sp.dma_start(qtl_nat[:], q_to_latent.rearrange("h d l -> (h d) l")).then_inc(s_w, 16)
            sp.dma_start(wkd[:], Wk_down).then_inc(s_w, 16)
            sp.dma_start(wg[:], w_gate).then_inc(s_w, 16)
            sp.dma_start(wvd[:], Wv_down).then_inc(s_w, 16)
            sp.dma_start(vup[:, 0:H // 2], v_up[0:H // 2].rearrange("h l d -> l h d")).then_inc(s_w, 16)
            sp.dma_start(vup[:, H // 2:H], v_up[H // 2:H].rearrange("h l d -> l h d")).then_inc(s_w, 16)

            def load_stacks(b, w):
                parts, rows, stack = parts_dram[w][b.buf], (Q_ROWS, K_ROWS)[w], (q_stack, k_stack)[w][b.buf]
                sp.wait_ge(s_parts, 2 * b.num + w + 1)
                for p in range(PARTS):
                    sp.dma_start(parts[p].rearrange("d h t -> h d t"), qk_parts[w][:, p, :]).then_inc(s_pst[w][b.buf], 16)
                sp.wait_ge(s_pst[w][b.buf], PARTS * 16 * (b.round + 1))
                sp.wait_ge(s_zero[b.buf], 3)
                wait(sp, s_sc, exps(b.plus(-STACK), QUADS - 1, EB - 1))
                for first, part, n in rows:
                    dst = stack[first * D:(first + n) * D].rearrange("p h t -> p (h t)")
                    if w == 0:
                        src = parts[part:part + 1].rearrange("o d h t -> o d (h t)").broadcast_to([n, D, H * T])
                    else:
                        src = parts[part:part + n].rearrange("o d h t -> (o d) (h t)")
                    sp.dma_start(dst, src).then_inc(s_stk[b.buf], 16)

            def step(b):
                done, prev, nxt, far = b.plus(-2), b.plus(-1), b.plus(1), b.plus(2)
                if far.exists:
                    wait(sp, s_xt, far.num - STACK + 1)
                    sp.dma_start(x_in[:, far.buf], x_dram[far.num]).then_inc(s_xin[far.buf], 16)
                if far.exists:
                    load_stacks(far, 0)
                if done.exists:
                    sp.wait_ge(s_x1, done.num + 1)
                    sp.dma_start(x1_v[done.num], image[:, :, 0, 0:E]).then_inc(s_out, 16)
                if prev.exists:
                    sp.dma_start(x_res[:, prev.buf], x_dram[prev.num]).then_inc(s_xres[prev.buf], 16)
                    sp.wait_ge(s_oc, quad(prev, QUADS - 1) + 1)
                    dst = heads_dram[prev.buf].rearrange("(g q) r t -> q r g t", q=QUAD)
                    for q in range(QUAD):
                        sp.dma_start(dst[q], heads_out[CT * q:CT * q + D + 1]).then_inc(s_hd[prev.buf], 16)
                    sp.wait_ge(s_hd[prev.buf], QUAD * 16 * (prev.round + 1))
                    wait(sp, s_ht, prev.num)
                    sp.dma_start(denom[:], heads_dram[prev.buf][:, D, :].rearrange("h (c t) -> h c t", c=D))\
                      .then_inc(s_nd[prev.buf], 16)
                    sp.dma_start(numer[:], heads_dram[prev.buf][:, 0:D, :]).then_inc(s_nd[prev.buf], 16)
                if far.exists:
                    load_stacks(far, 1)
                if prev.exists:
                    sp.wait_ge(s_rd, prev.num + 1)
                    sp.dma_start(recip_dram[prev.buf].rearrange("h (c t) -> h c t", c=D), rden[:])\
                      .then_inc(s_rst[prev.buf], 16)
                    sp.wait_ge(s_rst[prev.buf], 16 * (prev.round + 1))
                    sp.dma_start(rden_all[:],
                                 recip_dram[prev.buf].rearrange("h (o t) -> h o t", o=1).broadcast_to([H, D, T]))\
                      .then_inc(s_rl[prev.buf], 16)
                if nxt.exists:
                    sp.wait_ge(s_nmp, nxt.num + 1)
                    for p in range(PARTS):
                        sp.dma_start(q_stack[nxt.buf][MAX_ROW + p:MAX_ROW + p + 1].rearrange("o h (i t) -> o (h i) t", i=TT),
                                     max_parts[:, p, :]).then_inc(s_nmd[nxt.buf], 16)

            over_batches(sp, B, step)
            sp.wait_ge(s_out, 16 * B)

        @block.gpsimd
        def _(pool):
            pool.memset(ident[:], 0.0).then_inc(s_const, 1)
            pool.memset(ahead[:], 0.0).then_inc(s_const, 1)
            pool.wait_ge(s_const, 2)
            pool.affine_select(out=ident[:], in_=ident[:], compare_op=ALU.not_equal, fill=1.0, base=0,
                               pattern=[[-1, P]], channel_multiplier=1).then_inc(s_const, 1)
            pool.affine_select(out=ahead[:], in_=ahead[:], compare_op=ALU.is_ge, fill=NEG, base=0,
                               pattern=[[0, 2], [-1, P]], channel_multiplier=1).then_inc(s_const, 1)
            pool.wait_ge(s_const, 4)
            pool.tensor_copy(ident_bf[:], ident[:]).then_inc(s_const, 1)
            pool.memset(eps_col[:], EPS).then_inc(s_const, 1)
            pool.memset(ones_bf[:], 1.0).then_inc(s_const, 1)
            pool.memset(tmp_f[:], 1.0).then_inc(s_const, 1)
            pool.iota(iota_i[:], pattern=[[1, X]], base=0, channel_multiplier=0).then_inc(s_const, 1)
            pool.iota(dest_i[:], pattern=[[P, TT], [TOKENS, TOP]], base=0, channel_multiplier=1).then_inc(s_const, 1)
            pool.wait_ge(s_const, 10)
            pool.affine_select(out=tmp_f[:], in_=tmp_f[:], compare_op=ALU.is_gt, fill=0.0, base=0,
                               pattern=[[1, P]], channel_multiplier=-1).then_inc(s_const, 1)
            pool.wait_ge(s_const, 11)
            pool.tensor_copy(before[:], tmp_f[:]).then_inc(s_const, 1)
            for i in range(STACK):
                pool.memset(v_aug[:, i], 1.0).then_inc(s_vones, 1)
            for i in range(1, STACK):
                clear_stacks(pool, i)

            def step(b):
                for g in range(QUADS):
                    if b.exists:
                        for pr in range(HP):
                            k = 5 * pr
                            pt = probs[:, g % 2]
                            full = pt[:, k:k + 2, 0:P]
                            wait_apart(pool, s_exp, exps(b, g, k + 1), s_passed_pool)
                            pool.affine_select(out=full, in_=full, compare_op=ALU.is_ge, fill=0.0, base=0,
                                               pattern=[[0, 2], [1, P]], channel_multiplier=-1).then_inc(s_tri, 1)
                            odd = pt[:, k + 2:k + 4, 0:2 * P].rearrange("p e (i t) -> p e i t", i=2)
                            wait_apart(pool, s_exp, exps(b, g, k + 3), s_passed_pool)
                            pool.affine_select(out=odd, in_=odd, compare_op=ALU.is_ge, fill=0.0, base=0,
                                               pattern=[[0, 2], [0, 2], [1, P]], channel_multiplier=-1).then_inc(s_tri, 1)
                            both = pt[:, k + 4, :].rearrange("p (e t) -> p e t", e=2)[:, :, 0:P]
                            wait_apart(pool, s_exp, exps(b, g, k + 4), s_passed_pool)
                            pool.affine_select(out=both, in_=both, compare_op=ALU.is_ge, fill=0.0, base=0,
                                               pattern=[[0, 2], [1, P]], channel_multiplier=-1).then_inc(s_tri, 1)
                    far, prev, done = b.plus(2), b.plus(-1), b.plus(-2)
                    if g == 2 and done.exists:
                        wait_apart(pool, s_x1, done.num + 1, s_passed_pool)
                        pool.tensor_copy(image[:, :, 1, 0:E], image[:, :, 0, 0:E]).then_inc(s_im, 1)
                    if g == 3 and done.exists:
                        wait_apart(pool, s_rows, done.num + 1, s_passed_pool)
                        wait_apart(pool, s_im, done.num + 1, s_passed_pool)
                        for i in range(TT):
                            for j in range(TOP):
                                pool.indirect_dma_start(
                                    out=xs_dram, out_offset=bass.IndirectOffsetOnAxis(ap=row_i[:, i, j:j + 1], axis=0),
                                    in_=image[:, i, j, :], in_offset=None).then_inc(s_sct, 16)
                    if g < 2 and far.exists:
                        w = g
                        wait_apart(pool, s_rest, 2 * far.num + w + 1, s_passed_pool)
                        pool.tensor_copy(qk_parts[w][:, 1, :], qk_rest[w][:]).then_inc(s_mid, 1)
                        wait_apart(pool, s_mid, 2 * far.num + w + 1, s_passed_pool)
                        pool.tensor_tensor(qk_parts[w][:, 2, :], qk_rest[w][:], qk_parts[w][:, 1, :], ALU.subtract)\
                            .then_inc(s_parts, 1)
                    if g == 2 and prev.exists:
                        wait_apart(pool, s_rl[prev.buf], 16 * (prev.round + 1), s_passed_pool)
                        wait_apart(pool, s_nd[prev.buf], 2 * 16 * (prev.round + 1), s_passed_pool)
                        wait_apart(pool, s_op, prev.num, s_passed_pool)
                        pool.tensor_tensor(headsT[:], numer[:], rden_all[:], ALU.mult)\
                            .then_inc(s_ht, 1)

            over_batches(pool, B, step)
            pool.wait_ge(s_sct, TT * TOP * 16 * B)

        @block.tensor
        def _(pe):
            pe.wait_ge(s_w, WEIGHTS)
            pe.wait_ge(s_const, 3)
            pe.transpose(misc[:, 0:P], wq_nat[:], ident[:]).then_inc(s_wt, 1)
            pe.transpose(misc[:, P:2 * P], wout_nat[:], ident[:]).then_inc(s_wt, 1)
            pe.transpose(misc[0:L, 2 * P:3 * P], qtl_nat[:], ident[:]).then_inc(s_wt, 1)
            pe.wait_ge(s_wc, 3)
            pe.matmul(misc[:, 0:P], wkd[:], qtlT[:], start=True, stop=True).then_inc(s_wt, 1)
            pe.matmul(misc[:, P:2 * P], wvd[:], vup[:].rearrange("l h d -> l (h d)"), start=True, stop=True)\
              .then_inc(s_wt, 1)
            pe.wait_ge(s_wc, 5)

            pe.wait_ge(s_wc, 5)

            def score_unit(b, g, k):
                n = exps(b, g, k)
                if k == 0 and g == 0:
                    pe.wait_ge(s_nmd[b.buf], PARTS * 16 * (b.round + 1))
                wait(pe, s_exp, n - 2)
                bank, kk, pr = score[:, k % 2], k % 5, k // 5
                ks, qs = k_stack[b.buf], q_stack[b.buf]
                R = MAX_ROW + PARTS

                def mm(c0, j, h, start):
                    return pe.matmul(bank[:, c0:c0 + T - P * j], ks[0:R, h, P * j:P * j + P], qs[0:R, h, P * j:T],
                                     start=start, stop=True, skip_group_check=True)
                h0 = QUAD * g + 2 * pr
                if kk < 2:
                    last = mm(0, 0, h0 + kk, True)
                elif kk < 4:
                    mm(0, 3, h0 + kk - 2, True)
                    last = mm(P, 1, h0 + kk - 2, False)
                else:
                    mm(0, 2, h0, True)
                    last = mm(2 * P, 2, h0 + 1, False)
                last.then_inc(s_sc, 1)

            def max_bank(b, g, k):
                n = maxes(b, g, k // 2)
                if k == 0 and g == 0:
                    pe.wait_ge(s_stk[b.buf], 6 * 16 * (b.round + 1))
                if k % 2 == 0:
                    wait(pe, s_mx, n - 2)
                bank, kk, pr = maxs[:, (g * MB + k // 2) % 2, k % 2], k % 5, k // 5
                ks, qs = k_stack[b.buf], q_stack[b.buf]

                def mm(c0, i, h, start):
                    pe.matmul(bank[:, c0:c0 + P * (i + 1)], qs[0:MAX_ROW, h, P * i:P * i + P],
                              ks[0:MAX_ROW, h, 0:P * (i + 1)], start=start, stop=False, skip_group_check=True)

                def mask(cols, n):
                    return pe.matmul(cols, ident_bf[:], ahead[:, 0:n], start=False, stop=True, skip_group_check=True)
                h0 = QUAD * g + 2 * pr
                if kk < 2:
                    mm(0, 3, h0 + kk, True)
                    last = mask(bank[:, 3 * P:4 * P], 1)
                elif kk < 4:
                    mm(0, 2, h0 + kk - 2, True)
                    mm(3 * P, 0, h0 + kk - 2, False)
                    last = mask(bank[:, 2 * P:4 * P], 2)
                else:
                    mm(0, 1, h0, True)
                    mm(2 * P, 1, h0 + 1, False)
                    last = mask(bank.rearrange("p (e t) -> p e t", e=2)[:, :, P:2 * P], 2)
                if k % 2:
                    last.then_inc(s_msc, 1)

            def attend(b, g, j):
                if j == 0:
                    pe.wait_ge(s_tri, TRI * (quad(b, g) + 1))
                    wait(pe, s_oc, quad(b, g))
                    if g == 0:
                        pe.wait_ge(s_vc, b.num + 1)
                pt = probs[:, g % 2]
                for q in range(QUAD):
                    v0 = (j * H + QUAD * g + q) * 2 * D
                    pr, e = q // 2, q % 2
                    if j == 0:
                        src = pt[:, 5 * pr + e, :]
                    elif j == 1:
                        src = pt[:, 5 * pr + 2 + e, P:T]
                    elif j == 2:
                        src = pt[:, 5 * pr + 4, 2 * P * e:2 * P * (e + 1)]
                    else:
                        src = pt[:, 5 * pr + 2 + e, 0:P]
                    last = pe.matmul(attn[CT * q:CT * (q + 1), P * j:T], v_aug[:, b.buf, v0:v0 + CT], src,
                                     start=j == 0, stop=j == TT - 1)
                if j == TT - 1:
                    last.then_inc(s_pv, 1)

            def small(b, g, k):
                prev, nxt, far = b.plus(-1), b.plus(1), b.plus(2)
                done = b.plus(-2)
                if (g, k) == (0, 1) and far.exists:
                    pe.wait_ge(s_xin[far.buf], 16 * (far.round + 1))
                    wait(pe, s_vc, far.num)
                    wait(pe, s_nmr, b.num + 1)
                    wait(pe, s_rr, done.num)
                    wait(pe, s_res, done.num + 1)
                    for i in range(TT):
                        last = pe.transpose(misc[:, P * i:P * i + P], x_in[:, far.buf, i, :], ident[:])
                    last.then_inc(s_xt, 1)
                if (g, k) in ((0, 5), (0, 9)) and far.exists:
                    w = int(k == 9)
                    if w == 0:
                        pe.wait_ge(s_xtc, far.num + 1)
                    else:
                        pe.wait_ge(s_rest, 2 * far.num + w)
                    pe.matmul(misc[:], (wqT, wkT)[w][:], xT[:], start=True, stop=True).then_inc(s_proj, 1)
                if (g, k) == (1, 4) and far.exists:
                    pe.wait_ge(s_rest, 2 * far.num + 2)
                    for i in range(TT):
                        last = pe.matmul(misc[:, P * i:P * i + P], xT[:, P * i:P * i + P], wvT[:], start=True, stop=True)
                    last.then_inc(s_v, 1)
                if (g, k) == (1, 8) and done.exists:
                    pe.wait_ge(s_x1, done.num + 1)
                    if far.exists:
                        pe.wait_ge(s_vc, far.num + 1)
                    wait(pe, s_res, done.num + 1)
                    for i in range(TT):
                        last = pe.transpose(misc[:, P * i:P * i + P], image[:, i, 0, 0:E], ident[:])
                    last.then_inc(s_x1t, 1)
                if (g, k) == (2, 2) and done.exists:
                    pe.wait_ge(s_x1tc, done.num + 1)
                    for i in range(TT):
                        last = pe.matmul(misc[:, X * i:X * i + X], x1T[:, P * i:P * i + P], wg[:], start=True, stop=True)
                    last.then_inc(s_lg, 1)
                if (g, k) == (2, 8) and done.exists:
                    pe.wait_ge(s_oh, done.num + 1)
                    n = 0
                    for j in range(TOP):
                        ch = chosen_bf[:, :, j, :]
                        pe.matmul(misc[:, 0:TT * X].rearrange("p (i x) -> p i x", i=TT), before[:], ch, start=j == 0, stop=False,
                                  skip_group_check=True)
                        for s in range(1, TT):
                            pe.matmul(misc[:, s * X:TT * X].rearrange("p (i x) -> p i x", x=X), ones_bf[:], ch[:, 0:TT - s],
                                      start=False, stop=False, skip_group_check=True)
                        for i in range(TT):
                            last = pe.matmul(misc[:, TT * X:TT * X + X], ones_bf[:], ch[:, i], start=False, stop=True,
                                             skip_group_check=True)
                    last.then_inc(s_rk, 1)
                if (g, k) == (3, 2) and nxt.exists:
                    pe.wait_ge(s_rm, nxt.num + 1)
                    if far.exists:
                        pe.wait_ge(s_vc, far.num + 1)
                    wait(pe, s_rr, done.num + 1)
                    wait_apart(pe, s_res, prev.num, s_passed_pe)
                    pe.transpose(misc[0:H * TT, 0:P], row_max[:].rearrange("p h i -> p (h i)"), ident[:]).then_inc(s_nmt, 1)
                if (g, k) == (3, 6) and prev.exists:
                    if nxt.exists:
                        pe.wait_ge(s_nmr, nxt.num + 1)
                    wait(pe, s_rr, done.num + 1)
                    wait(pe, s_res, prev.num)
                    pe.wait_ge(s_ht, prev.num + 1)
                    for i in range(TT):
                        last = pe.matmul(misc[:, P * i:P * i + P], headsT[:, P * i:P * i + P], woutT[:], start=True, stop=True)
                    last.then_inc(s_op, 1)

            def step(b):
                for g in range(QUADS):
                    mb, mg = (b.plus(1), g + 1) if g + 1 < QUADS else (b.plus(2), 0)
                    pb, pg = (b, g - 1) if g else (b.plus(-1), QUADS - 1)
                    for k in range(EB):
                        if b.exists:
                            score_unit(b, g, k)
                        small(b, g, k)
                        if mb.exists:
                            max_bank(mb, mg, k)
                        if pb.exists and k % 2 and k > 1:
                            attend(pb, pg, k // 2 - 1)

            over_batches(pe, B, step)

        @block.scalar
        def _(act):
            act.preload_act_table_set("natural_log_exp_and_others")

            def step(b):
                prev, nxt, far, done = b.plus(-1), b.plus(1), b.plus(2), b.plus(-2)
                for g in range(QUADS):
                    ob, og = (b, g - 2) if g >= 2 else (b.plus(-1), g + QUADS - 2)
                    for k in range(EB):
                        if b.exists:
                            if k == 0:
                                wait(act, s_pv, quad(b, g) - 1)
                            act.wait_ge(s_sc, exps(b, g, k))
                            act.activation(probs[:, g % 2, k, :], score[:, k % 2], ACT.Exp).then_inc(s_exp, 1)
                        if (g, k) == (0, 2) and far.exists:
                            act.wait_ge(s_xt, far.num + 1)
                            wait(act, s_v, far.num)
                            act.activation(xT[:], misc[:], ACT.Copy).then_inc(s_xtc, 1)
                        if (g, k) in ((0, 6), (1, 0)) and far.exists:
                            w = g
                            act.wait_ge(s_proj, 2 * far.num + w + 1)
                            before = far.plus(-1)
                            wait(act, s_pst[w][before.buf], PARTS * 16 * (before.round + 1))
                            act.activation(qk_parts[w][:, 0, :], misc[:], ACT.Copy).then_inc(s_hi, 1)
                        if ob.exists and k == 1 and og % 2 == 0:
                            act.wait_ge(s_pv, quad(ob, og) + 1)
                            if og == 0:
                                before = ob.plus(-1)
                                wait(act, s_hd[before.buf], QUAD * 16 * (before.round + 1))
                            act.activation(heads_out[:, og], attn[:], ACT.Copy).then_inc(s_oc, 1)
                        if (g, k) == (3, 3) and nxt.exists:
                            act.wait_ge(s_nmt, nxt.num + 1)
                            wait(act, s_nmd[b.buf], PARTS * 16 * (b.round + 1))
                            act.activation(max_parts[:, 0, :], misc[0:H * TT, 0:P], ACT.Copy, scale=-1.0).then_inc(s_nm0, 1)
                        if (g, k) == (1, 9) and done.exists:
                            act.wait_ge(s_x1t, done.num + 1)
                            act.activation(x1T[:], misc[:], ACT.Copy).then_inc(s_x1tc, 1)
                        if (g, k) == (2, 7) and done.exists:
                            act.wait_ge(s_gap, done.num + 1)
                            act.activation(odds[:], gap[:], ACT.Exp).then_inc(s_odds, 1)
                        if (g, k) == (0, 1) and done.exists:
                            act.wait_ge(s_st, 2 * (done.num + 1))
                            act.activation(log_var[:], mean_var[:, :, 1], ACT.Ln, bias=eps_col[:]).then_inc(s_ln, 1)
                            act.wait_ge(s_ln, done.num + 1)
                            act.activation(rstd[:], log_var[:], ACT.Exp, scale=-0.5).then_inc(s_rs, 1)

            act.wait_ge(s_const, 6)
            over_batches(act, B, step)

        @block.vector
        def _(dve):
            clear_stacks(dve, 0)
            for n, (dst, src, scale) in enumerate([
                (wqT[:], misc[:, 0:P], SC), (woutT[:], misc[:, P:2 * P], 1.0), (qtlT[:], misc[0:L, 2 * P:3 * P], 1.0),
                (wkT[:], misc[:, 0:P], 1.0), (wvT[:], misc[:, P:2 * P], 1.0),
            ]):
                dve.wait_ge(s_wt, 3 if n < 3 else 5)
                dve.tensor_scalar_mul(dst, src, scale).then_inc(s_wc, 1)

            dve.wait_ge(s_const, 12)
            dve.tensor_copy(iota_x[:], iota_i[:]).then_inc(s_ch, 1)
            dve.tensor_copy(dest[:].rearrange("p i j -> p (i j)"), dest_i[:]).then_inc(s_ch, 1)
            dve.wait_ge(s_ch, 2)
            dve.tensor_scalar_mul(region0[:], iota_x[:], float(REGION)).then_inc(s_ch, 1)
            dve.tensor_scalar_mul(base[:], iota_x[:], float(REGION)).then_inc(s_ch, 1)
            CHOICE, PLACE = 4, 8

            def choose(b):
                n = 4 + CHOICE * b.num
                dve.wait_ge(s_lg, b.num + 1)
                dve.tensor_copy(logits[:].rearrange("p i x -> p (i x)"), misc[:, 0:TT * X]).then_inc(s_ch, 1)
                wait_apart(dve, s_ch, n + 1, s_passed_dve)
                for i in range(TT):
                    last = dve.max(top[:, i], logits[:, i])
                last.then_inc(s_ch, 1)
                dve.wait_ge(s_ch, n + 2)
                dve.tensor_tensor(gap[:], top[:, :, 1], top[:, :, 0], ALU.subtract).then_inc(s_gap, 1)
                for i in range(TT):
                    last = dve.max_index(top_at[:, i], top[:, i], logits[:, i])
                last.then_inc(s_ch, 1)
                dve.wait_ge(s_ch, n + 3)
                dve.tensor_copy(top_f[:], top_at[:, :, 0:TOP]).then_inc(s_ch, 1)
                dve.wait_ge(s_ch, n + 4)
                dve.tensor_tensor(chosen_bf[:].rearrange("p i j x -> p (i j) x"),
                                  iota_x[:].rearrange("p (o x) -> p o x", o=1).to_broadcast([P, TT * TOP, X]),
                                  top_f[:].rearrange("p i (j o) -> p (i j) o", o=1).to_broadcast([P, TT * TOP, X]),
                                  ALU.is_equal).then_inc(s_oh, 1)

            def place(b):
                n = PLACE * b.num
                dve.wait_ge(s_rk, b.num + 1)
                dve.tensor_tensor(row_of[:], misc[:, 0:TT * X].rearrange("p (i x) -> p i x", x=X),
                                  base[:].rearrange("p (o x) -> p o x", o=1).to_broadcast([P, TT, X]), ALU.add).then_inc(s_ro, 1)
                dve.wait_ge(s_ro, n + 1)
                dve.tensor_tensor(base[:], base[:], misc[:, TT * X:TT * X + X], ALU.add).then_inc(s_rr, 1)
                for j in range(TOP):
                    last = dve.tensor_tensor(picked[:, :, j], row_of[:], chosen_bf[:, :, j], ALU.mult)
                last.then_inc(s_ro, 1)
                dve.wait_ge(s_ro, n + 2)
                dve.tensor_reduce(row_f[:].rearrange("p i j -> p (i j)"), picked[:].rearrange("p i j x -> p (i j) x"),
                                  AX.X, ALU.add).then_inc(s_ro, 1)
                dve.wait_ge(s_odds, b.num + 1)
                dve.tensor_scalar_add(odds1[:], odds[:], 1.0).then_inc(s_ro, 1)
                dve.wait_ge(s_ro, n + 4)
                dve.reciprocal(image[:, :, 0, E], odds1[:]).then_inc(s_ro, 1)
                dve.wait_ge(s_ro, n + 5)
                dve.tensor_tensor(image[:, :, 1, E], odds[:], image[:, :, 0, E], ALU.mult).then_inc(s_ro, 1)
                dve.tensor_copy(image[:, :, :, E + 1], dest[:]).then_inc(s_ro, 1)
                dve.wait_ge(s_ro, n + 7)
                dve.tensor_scalar_add(dest[:], dest[:], float(T)).then_inc(s_ro, 1)
                dve.wait_ge(s_ro, n + 8)
                dve.tensor_copy(row_i[:], row_f[:]).then_inc(s_rows, 1)

            def max_unit(b, g, m):
                dve.wait_ge(s_msc, maxes(b, g, m))
                flat = part_max[:].rearrange("p a k i -> p (a k i)")
                first = (g * MB + m) * 8
                if m == 0 and g == 0:
                    wait(dve, s_rm, b.num)
                dve.tensor_reduce(flat[:, first:first + 8],
                                  maxs[:, (g * MB + m) % 2].rearrange("p c (i t) -> p (c i) t", t=P), AX.X, ALU.max)\
                   .then_inc(s_mx, 1)

            def step(b):
                prev, nxt, far, done = b.plus(-1), b.plus(1), b.plus(2), b.plus(-2)
                for g in range(QUADS):
                    mb, mg = (b.plus(1), g + 1) if g + 1 < QUADS else (b.plus(2), 0)
                    ob, og = (b, g - 2) if g >= 2 else (b.plus(-1), g + QUADS - 2)
                    for m in range(MB):
                        if mb.exists:
                            max_unit(mb, mg, m)
                        if ob.exists and m == 0 and og % 2 == 1:
                            dve.wait_ge(s_pv, quad(ob, og) + 1)
                            dve.tensor_copy(heads_out[:, og], attn[:]).then_inc(s_oc, 1)
                        if (g, m) in ((0, 3), (1, 0)) and far.exists:
                            w = g
                            dve.wait_ge(s_hi, 2 * far.num + w + 1)
                            dve.tensor_tensor(qk_rest[w][:], misc[:], qk_parts[w][:, 0, :], ALU.subtract).then_inc(s_rest, 1)
                        if (g, m) == (1, 3) and far.exists:
                            dve.wait_ge(s_v, far.num + 1)
                            dve.wait_ge(s_vones, far.buf + 1)
                            wait(dve, s_pv, quad(far.plus(-STACK), QUADS - 1) + 1)
                            v_rows = v_aug[:, far.buf, 0:TT * H * 2 * D].rearrange("p (n d) -> p n d", d=2 * D)
                            dve.tensor_copy(v_rows[:, :, 0:D], misc[:].rearrange("p (n d) -> p n d", d=D))\
                               .then_inc(s_vc, 1)
                        if (g, m) == (2, 1) and done.exists:
                            choose(done)
                        if (g, m) == (3, 0) and done.exists:
                            place(done)
                        if (g, m) == (2, 0) and prev.exists:
                            dve.wait_ge(s_nd[prev.buf], 2 * 16 * (prev.round + 1))
                            dve.reciprocal(rden[:], denom[:]).then_inc(s_rd, 1)
                        if (g, m) == (3, 4) and prev.exists:
                            dve.wait_ge(s_op, prev.num + 1)
                            dve.wait_ge(s_xres[prev.buf], 16 * (prev.round + 1))
                            wait(dve, s_x1, prev.num)
                            dve.tensor_tensor(resid[:].rearrange("p i e -> p (i e)"), misc[:],
                                              x_res[:, prev.buf].rearrange("p i e -> p (i e)"), ALU.add).then_inc(s_res, 1)
                            dve.wait_ge(s_res, prev.num + 1)
                            for i in range(TT):
                                last = dve.bn_stats(stats[:, i], resid[:, i])
                            last.then_inc(s_st, 1)
                            wait_apart(dve, s_st, 2 * prev.num + 1, s_passed_dve)
                            for i in range(TT):
                                last = dve.bn_aggr(mean_var[:, i], stats[:, i])
                            last.then_inc(s_st, 1)
                        if (g, m) == (0, 1) and done.exists:
                            dve.wait_ge(s_rs, done.num + 1)
                            wait(dve, s_out, 16 * done.num)
                            wait(dve, s_sct, TT * TOP * 16 * done.num)
                            for i in range(TT):
                                last = dve.tensor_scalar(image[:, i, 0, 0:E], resid[:, i], mean_var[:, i, 0:1],
                                                         rstd[:, i:i + 1], ALU.subtract, ALU.mult)
                            last.then_inc(s_x1, 1)
                        if (g, m) == (3, 2) and nxt.exists:
                            dve.wait_ge(s_nm0, nxt.num + 1)
                            dve.scalar_tensor_tensor(out=max_rest[:], in0=misc[0:H * TT, 0:P], scalar=-1.0,
                                                     in1=max_parts[:, 0, :], op0=ALU.mult, op1=ALU.subtract).then_inc(s_nmr, 1)
                            dve.wait_ge(s_nmr, nxt.num + 1)
                            dve.tensor_copy(max_parts[:, 1, :], max_rest[:]).then_inc(s_nm1, 1)
                            dve.wait_ge(s_nm1, nxt.num + 1)
                            dve.tensor_tensor(max_parts[:, 2, :], max_rest[:], max_parts[:, 1, :], ALU.subtract)\
                               .then_inc(s_nmp, 1)
                    if g == 2 and nxt.exists:
                        pm = part_max[:]
                        dve.wait_ge(s_mx, maxes(nxt, QUADS - 1, MB - 1))
                        wait(dve, s_nmt, nxt.num)
                        rm = row_max[:].rearrange("p (a e) i -> p a e i", e=2)
                        dve.tensor_reduce(rm[:, :, :, 3], pm[:, :, 0:2, :], AX.X, ALU.max)
                        dve.tensor_reduce(rm[:, :, :, 2], pm[:, :, 2:4, 0:3], AX.X, ALU.max)
                        dve.tensor_reduce(rm[:, :, :, 1], pm[:, :, 4, :].rearrange("p a (e i) -> p a e i", e=2), AX.X, ALU.max)
                        dve.tensor_copy(rm[:, :, :, 0], pm[:, :, 2:4, 3]).then_inc(s_rm, 1)

            over_batches(dve, B, step)



    experts(nc, B, T, E, X, F, REGION, ROW, SPARE, JOBS, NOWHERE, w1, w3, w2, xs_dram, y_dram, x1_dram, out,
            base, region0, ident, eps_col)
    keep.close()


def experts(nc, B, T, E, X, F, REGION, ROW, SPARE, JOBS, NOWHERE, w1, w3, w2, xs_dram, y_dram, x1_dram, out,
            base, region0, ident, eps_col):
    TT = T // P
    TOP = 2
    FC = F // P
    TOKENS = B * T
    XR = 4
    YR = 4
    ctx = ExitStack()
    with ctx:
        def sb(name, shape, dt=FP32):
            return ctx.enter_context(nc.sbuf_tensor(name, shape, dt))

        def ps(name, shape, dt=FP32):
            return ctx.enter_context(nc.psum_tensor(name, shape, dt))

        def sem(name):
            return ctx.enter_context(nc.semaphore(name))

        def sems(name, n):
            return [sem(f"{name}{i}") for i in range(n)]

        w13 = sb("w13", [P, X, 2 * F])
        w2s = sb("w2s", [P, X, FC, E])
        iota_pi = sb("iota_pi", [P, 1], INT32)
        iota_p = sb("iota_p", [P, 1])
        iota_ji = sb("iota_ji", [P, JOBS], INT32)
        iota_j = sb("iota_j", [P, JOBS])
        rows_n = sb("rows_n", [P, X])
        tiles_i = sb("tiles_i", [P, X], INT32)
        tiles = sb("tiles", [P, X])
        ones_x = sb("ones_x", [P, X])
        tile_end = sb("tile_end", [P, X])
        tile_start = sb("tile_start", [P, X])
        lead = sb("lead", [P, X])
        past_end = sb("past_end", [1, JOBS, X])
        past_start = sb("past_start", [1, JOBS, X])
        inside = sb("inside", [1, JOBS, X])
        first = sb("first", [1, JOBS, X])
        job_xf = sb("job_xf", [1, JOBS])
        job_rf = sb("job_rf", [1, JOBS])
        job_sf = sb("job_sf", [1, JOBS])
        job_x = sb("job_x", [1, JOBS], INT32)
        job_row = sb("job_row", [1, JOBS], INT32)
        pad_f = sb("pad_f", [P, X])
        pad_i = sb("pad_i", [P, X], UINT32)
        padding = sb("padding", [P, ROW])
        rows = sb("rows", [P, XR, ROW])
        rowsT = sb("rowsT", [E, 2, P])
        gate = sb("gate", [P, 2, F])
        hid = sb("hid", [P, 2, F])
        hidT = sb("hidT", [P, 2, FC, P])
        res = sb("res", [P, YR, E])
        res_to = sb("res_to", [P, YR], UINT32)
        NB = 3
        xa = sb("xa", [P, NB, TT, E])
        ya = sb("ya", [P, NB, TOP, TT, E])
        yy = sb("yy", [P, TT, E])
        tot = sb("tot", [P, 2, TT, E])
        stats = sb("stats2", [P, TT, 6])
        mean_var = sb("mean_var2", [P, 2, TT, 2])
        log_var = sb("log_var2", [P, TT])
        rstd = sb("rstd2", [P, 2, TT])
        fin = sb("fin", [P, 2, TT, E])

        psX = ps("psX", [P, 2, T])
        psH = ps("psH", [P, 2, T])
        psT = ps("psT", [P, 2, T])
        psY = ps("psY", [P, 2, T])

        s_passed_pool = sem("pool_passed2")
        s_w = sem("expert_weights_loaded")
        s_io = sem("iotas_made")
        s_pl = sem("plan_step")
        s_plan = sem("plan_made")
        s_pad = sem("padding_stored")
        s_spare = sem("spare_stored")
        s_x = sems("rows_loaded", XR)
        s_xt = sem("rows_transposed")
        s_xc = sem("rowsT_copied")
        s_h = sem("hidden_ready")
        s_g = sem("gate_made")
        s_m = sem("hidden_made")
        s_ht = sem("hidden_transposed")
        s_hc = sem("hiddenT_copied")
        s_y = sem("result_ready")
        s_to = sem("destination_made")
        s_yc = sem("result_scaled")
        s_sc = sems("result_scattered", YR)
        s_l = sems("sum_inputs_loaded", NB)
        s_a1 = sem("results_added")
        s_a2 = sem("total_made")
        s_st = sem("stats_made2")
        s_mv = sem("mean_var_made2")
        s_lg = sem("log_made2")
        s_rs = sem("rstd_made2")
        s_f = sem("final_made")
        s_o = sems("out_stored", 2)

        x_v = x1_dram.rearrange("(b i p) e -> b p i e", p=P, i=TT)
        y_v = y_dram.rearrange("(j b i p) e -> j b p i e", p=P, i=TT, j=TOP)
        o_v = out.rearrange("b (i p) e -> b p i e", p=P)

        def over_jobs(eng, step, lead, lag):
            lo, hi = 2 * XR, JOBS - XR
            for n in range(-lead, lo):
                step(n, n % XR)
            with eng.Fori(0, (hi - lo) // XR) as i:
                for u in range(XR):
                    step(i * XR + lo + u, u)
            for n in range(lo + (hi - lo) // XR * XR, JOBS + lag):
                step(n, n % XR)

        def is_job(n):
            return not isinstance(n, int) or 0 <= n < JOBS

        block = ctx.enter_context(nc.Block())

        @block.sync
        def _(sp):
            sp.dma_start(w13[:, :, 0:F], w1.rearrange("x e f -> e x f")).then_inc(s_w, 16)
            sp.dma_start(w13[:, :, F:2 * F], w3.rearrange("x e f -> e x f")).then_inc(s_w, 16)
            sp.dma_start(w2s[:].rearrange("p x c e -> p (x c) e"), w2.rearrange("x (c p) e -> p (x c) e", p=P)).then_inc(s_w, 16)
            sp.wait_ge(s_plan, 1)
            sp.wait_ge(s_pad, 16 * X)
            sp.wait_ge(s_spare, 16)

            def step(n, u):
                if is_job(n):
                    wait(sp, s_yc, n - XR + 1)
                    row = sp.value_load(job_row[0:1, bass.ds(n, 1)], min_val=0, max_val=SPARE)
                    sp.dma_start(rows[:, u, :], xs_dram[bass.ds(row, P), :]).then_inc(s_x[u], 16)

            over_jobs(sp, step, 0, 0)
            for u in range(YR):
                sp.wait_ge(s_sc[u], 16 * len(range(u, JOBS, YR)))

            def load(b):
                u = b % NB
                wait(sp, s_a2, b - NB + 1)
                sp.dma_start(xa[:, u], x_v[b]).then_inc(s_l[u], 16)
                for j in range(TOP):
                    sp.dma_start(ya[:, u, j], y_v[j, b]).then_inc(s_l[u], 16)
            for b in range(NB):
                load(b)
            for b in range(B):
                sp.wait_ge(s_f, b + 1)
                sp.dma_start(o_v[b], fin[:, b % 2]).then_inc(s_o[b % 2], 16)
                if b + NB < B:
                    load(b + NB)
            for u in range(2):
                sp.wait_ge(s_o[u], 16 * len(range(u, B, 2)))

        @block.gpsimd
        def _(pool):
            pool.iota(iota_pi[:], pattern=[[0, 1]], base=0, channel_multiplier=1).then_inc(s_io, 1)
            pool.iota(iota_ji[:], pattern=[[1, JOBS]], base=0, channel_multiplier=0).then_inc(s_io, 1)
            pool.memset(padding[:], 0.0).then_inc(s_io, 1)
            pool.wait_ge(s_io, 3)
            pool.memset(padding[:, E + 1:E + 2], NOWHERE).then_inc(s_io, 1)
            pool.wait_ge(s_io, 4)
            pool.dma_start(xs_dram[SPARE:SPARE + P, :], padding[:]).then_inc(s_spare, 16)
            pool.wait_ge(s_plan, 1)
            for x in range(X):
                pool.indirect_dma_start(out=xs_dram, out_offset=bass.IndirectOffsetOnAxis(ap=pad_i[:, x:x + 1], axis=0),
                                        in_=padding[:], in_offset=None).then_inc(s_pad, 16)

            def step(n, u):
                if is_job(n):
                    wait_apart(pool, s_yc, n + 1, s_passed_pool)
                    wait_apart(pool, s_to, n + 1, s_passed_pool)
                    pool.indirect_dma_start(out=y_dram, out_offset=bass.IndirectOffsetOnAxis(ap=res_to[:, u:u + 1], axis=0),
                                            in_=res[:, u, :], in_offset=None, bounds_check=TOP * TOKENS - 1,
                                            oob_is_err=False).then_inc(s_sc[u], 16)
            over_jobs(pool, step, 0, 0)

            for b in range(B):
                pool.wait_ge(s_l[b % NB], 48 * (b // NB + 1))
                wait(pool, s_a2, b)
                pool.tensor_tensor(yy[:], ya[:, b % NB, 0], ya[:, b % NB, 1], ALU.add).then_inc(s_a1, 1)

        @block.tensor
        def _(pe):
            pe.wait_ge(s_w, 48)
            pe.wait_ge(s_plan, 1)

            def step(n, u):
                v = u % 2
                ahead, back, back2 = n + 1, n - 1, n - 2
                if is_job(ahead):
                    pe.wait_ge(s_x[(u + 1) % XR], rounds(ahead, u + 1))
                    wait(pe, s_xc, ahead - 1)
                    pe.transpose(psX[:, (u + 1) % 2, 0:P], rows[:, (u + 1) % XR, 0:E], ident[:]).then_inc(s_xt, 1)
                if is_job(n):
                    x = pe.value_load(job_x[0:1, bass.ds(n, 1)], min_val=0, max_val=X - 1)
                    pe.wait_ge(s_xc, n + 1)
                    wait(pe, s_m, n - 1)
                    pe.matmul(psH[:, v, :], rowsT[:, v, :], w13[:, bass.ds(x, 1), :].rearrange("p o f -> p (o f)"),
                              start=True, stop=True).then_inc(s_h, 1)
                if is_job(back):
                    pe.wait_ge(s_m, back + 1)
                    wait(pe, s_hc, back - 1)
                    for c in range(FC):
                        last = pe.transpose(psT[:, 1 - v, P * c:P * c + P], hid[:, 1 - v, P * c:P * c + P], ident[:])
                    last.then_inc(s_ht, 1)
                if is_job(back2):
                    x2 = pe.value_load(job_x[0:1, bass.ds(back2, 1)], min_val=0, max_val=X - 1)
                    pe.wait_ge(s_hc, back2 + 1)
                    wait(pe, s_yc, back2 - 1)
                    for c in range(FC):
                        last = pe.matmul(psY[:, v, 0:E], hidT[:, v, c, :], w2s[:, bass.ds(x2, 1), c, :].rearrange("p o e -> p (o e)"),
                                         start=c == 0, stop=c == FC - 1)
                    last.then_inc(s_y, 1)

            def rounds(n, u):
                if isinstance(n, int):
                    return 16 * (n // XR + 1)
                return (n - (u % XR)) * (16 // XR) + 16
            over_jobs(pe, step, 1, 2)

        @block.scalar
        def _(act):
            act.preload_act_table(ACT.Silu)

            def step(n, u):
                v = u % 2
                ahead, back2 = n + 1, n - 2
                if is_job(ahead):
                    act.wait_ge(s_xt, ahead + 1)
                    wait(act, s_h, ahead - 1)
                    act.activation(rowsT[:, (u + 1) % 2, :], psX[:, (u + 1) % 2, 0:P], ACT.Copy).then_inc(s_xc, 1)
                if is_job(n):
                    act.wait_ge(s_h, n + 1)
                    wait(act, s_m, n - 1)
                    act.activation(gate[:, v, :], psH[:, v, 0:F], ACT.Silu).then_inc(s_g, 1)
                if is_job(back2):
                    w = (u - 2) % YR
                    act.wait_ge(s_y, back2 + 1)
                    if not isinstance(back2, int) or back2 >= YR:
                        act.wait_ge(s_sc[w], rounds(back2, w) - 16)
                    act.activation(res[:, w, :], psY[:, v, 0:E], ACT.Copy, scale=rows[:, w, E:E + 1]).then_inc(s_yc, 1)

            def rounds(n, u):
                if isinstance(n, int):
                    return 16 * (n // YR + 1)
                return (n - (u % YR)) * (16 // YR) + 16
            over_jobs(act, step, 1, 2)
            act.preload_act_table_set("natural_log_exp_and_others")
            for b in range(B):
                act.wait_ge(s_mv, b + 1)
                wait(act, s_rs, b)
                act.activation(log_var[:], mean_var[:, b % 2, :, 1], ACT.Ln, bias=eps_col[:]).then_inc(s_lg, 1)
                act.wait_ge(s_lg, b + 1)
                act.activation(rstd[:, b % 2], log_var[:], ACT.Exp, scale=-0.5).then_inc(s_rs, 1)

        @block.vector
        def _(dve):
            done = [0]

            def link(ins):
                done[0] += 1
                ins.then_inc(s_pl, 1)
                dve.wait_ge(s_pl, done[0])

            def along(ap):
                return ap.rearrange("p (o x) -> p o x", o=1).to_broadcast([1, JOBS, X])

            def across(ap):
                return ap.rearrange("p (j o) -> p j o", o=1).to_broadcast([1, JOBS, X])

            dve.wait_ge(s_io, 4)
            link(dve.tensor_copy(iota_p[:], iota_pi[:]))
            link(dve.tensor_copy(iota_j[:], iota_ji[:]))
            link(dve.memset(ones_x[:], 1.0))
            link(dve.tensor_tensor(rows_n[:], base[:], region0[:], ALU.subtract))
            link(dve.tensor_scalar_add(rows_n[:], rows_n[:], float(P - 1)))
            link(dve.tensor_copy(tiles_i[:], rows_n[:]))
            link(dve.tensor_single_scalar(tiles_i[:], tiles_i[:], P.bit_length() - 1, ALU.arith_shift_right))
            link(dve.tensor_copy(tiles[:], tiles_i[:]))
            link(dve.tensor_tensor_scan(tile_end[:], ones_x[:], tiles[:], 0.0, ALU.mult, ALU.add))
            link(dve.tensor_tensor(tile_start[:], tile_end[:], tiles[:], ALU.subtract))
            link(dve.tensor_scalar_mul(lead[:], tile_start[:], -float(P)))
            link(dve.tensor_tensor(lead[:], lead[:], region0[:], ALU.add))
            link(dve.tensor_tensor(past_end[:], across(iota_j[0:1, :]), along(tile_end[0:1, :]), ALU.is_ge))
            link(dve.tensor_tensor(past_start[:], across(iota_j[0:1, :]), along(tile_start[0:1, :]), ALU.is_ge))
            link(dve.tensor_tensor(inside[:], past_start[:], past_end[:], ALU.subtract))
            link(dve.tensor_scalar_mul(job_sf[:], iota_j[0:1, :], float(P)))
            link(dve.tensor_tensor(first[:], across(job_sf[:]), along(lead[0:1, :]), ALU.add))
            link(dve.tensor_tensor(first[:], first[:], inside[:], ALU.mult))
            link(dve.tensor_reduce(job_rf[:], first[:], AX.X, ALU.add))
            link(dve.tensor_reduce(job_xf[:], past_end[:], AX.X, ALU.add))
            link(dve.tensor_scalar_min(job_xf[:], job_xf[:], float(X - 1)))
            link(dve.tensor_scalar_mul(job_sf[:], past_end[:, :, X - 1], float(SPARE)))
            link(dve.tensor_tensor(job_rf[:], job_rf[:], job_sf[:], ALU.add))
            link(dve.tensor_copy(job_x[:], job_xf[:]))
            link(dve.tensor_copy(job_row[:], job_rf[:]))
            link(dve.tensor_scalar(pad_f[:], base[:], iota_p[:], None, ALU.add))
            dve.tensor_copy(pad_i[:], pad_f[:]).then_inc(s_plan, 1)

            def step(n, u):
                v = u % 2
                back = n - 1
                if is_job(n):
                    w = u % YR
                    if not isinstance(n, int) or n >= YR:
                        dve.wait_ge(s_sc[w], rounds(n, w) - 16)
                    dve.wait_ge(s_h, n + 1)
                    dve.tensor_copy(res_to[:, w:w + 1], rows[:, u, E + 1:E + 2]).then_inc(s_to, 1)
                    dve.wait_ge(s_g, n + 1)
                    wait(dve, s_ht, n - 1)
                    dve.tensor_tensor(hid[:, v, :], gate[:, v, :], psH[:, v, F:2 * F], ALU.mult).then_inc(s_m, 1)
                if is_job(back):
                    dve.wait_ge(s_ht, back + 1)
                    wait(dve, s_y, back - 1)
                    dve.tensor_copy(hidT[:, 1 - v].rearrange("p c t -> p (c t)"), psT[:, 1 - v, 0:F]).then_inc(s_hc, 1)

            def rounds(n, u):
                if isinstance(n, int):
                    return 16 * (n // YR + 1)
                return (n - (u % YR)) * (16 // YR) + 16
            over_jobs(dve, step, 0, 1)

            def total(b):
                dve.wait_ge(s_a1, b + 1)
                wait(dve, s_f, b - 1)
                dve.tensor_tensor(tot[:, b % 2], xa[:, b % NB], yy[:], ALU.add).then_inc(s_a2, 1)
                dve.wait_ge(s_a2, b + 1)
                for i in range(TT):
                    last = dve.bn_stats(stats[:, i], tot[:, b % 2, i])
                last.then_inc(s_st, 1)
                dve.wait_ge(s_st, b + 1)
                for i in range(TT):
                    last = dve.bn_aggr(mean_var[:, b % 2, i], stats[:, i])
                last.then_inc(s_mv, 1)

            def normalize(b):
                dve.wait_ge(s_rs, b + 1)
                if b >= 2:
                    dve.wait_ge(s_o[b % 2], 16 * (b // 2))
                for i in range(TT):
                    last = dve.tensor_scalar(fin[:, b % 2, i], tot[:, b % 2, i], mean_var[:, b % 2, i, 0:1],
                                             rstd[:, b % 2, i:i + 1], ALU.subtract, ALU.mult)
                last.then_inc(s_f, 1)

            for b in range(B):
                total(b)
                if b:
                    normalize(b - 1)
            normalize(B - 1)


_INS = ["L0_attn_hidden_states", "L0_attn_Wq", "L0_attn_Wk_down", "L0_attn_Wv_down", "L0_attn_q_to_latent",
        "L0_attn_v_up", "L0_attn_Wout", "L0_ffn_w_gate", "L0_ffn_w1", "L0_ffn_w3", "L0_ffn_w2"]


def kernel(**inputs):
    import numpy as _np
    import concourse.bacc as _bacc
    from concourse.bass_utils import run_bass_kernel_spmd as _run

    nc = _bacc.Bacc("TRN2", target_bir_lowering=False, num_devices=1)
    arrays, args = {}, []
    for name in _INS:
        a = _np.ascontiguousarray(inputs[name])
        arrays[f"in_{name}_dram"] = a
        args.append(nc.dram_tensor(f"in_{name}_dram", a.shape, mybir.dt.from_np(a.dtype), kind="ExternalInput").ap())
    shape = inputs[_INS[0]].shape
    out = nc.dram_tensor("out_dram", shape, FP32, kind="ExternalOutput").ap()
    build(nc, *args, out)
    r = _run(nc, [arrays], core_ids=[0])
    return r.results[0]["out_dram"]
```

```python
import concourse.bass as bass
from concourse import mybir
from contextlib import ExitStack

FP32 = mybir.dt.float32
BF16 = mybir.dt.bfloat16
INT32 = mybir.dt.int32
UINT32 = mybir.dt.uint32
ALU = mybir.AluOpType
ACT = mybir.ActivationFunctionType
AX = mybir.AxisListType

P = 128
NEG = -1e30
EPS = 1e-5
PARTS = 3
Q_ROWS = [(0, 0, 3), (3, 1, 2), (5, 2, 1)]
K_ROWS = [(0, 0, 3), (3, 0, 2), (5, 0, 1)]
SLOTS = 6
MAX_ROW = 96
STACK = 3


class Batch:

    def __init__(self, turns, off, count):
        self.turns, self.off, self.count = turns, off, count
        self.num = turns * STACK + off
        self.buf = off % STACK
        self.round = turns + off // STACK

    def plus(self, k):
        return Batch(self.turns, self.off + k, self.count)

    @property
    def exists(self):
        return not isinstance(self.num, int) or 0 <= self.num < self.count


def wait(eng, sem, value):
    if not isinstance(value, int) or value > 0:
        eng.wait_ge(sem, value)


def wait_apart(eng, sem, value, passed):
    if not isinstance(value, int):
        eng.wait_ge(sem, value)
        eng.sem_inc(passed, 1)
    elif value > 0:
        eng.wait_ge(sem, value)


def over_batches(eng, count, step):
    full_from, full_to = 3, count - 2
    turns = (full_to - full_from) // STACK
    for b in range(-2, full_from):
        step(Batch(0, b, count))
    if turns:
        with eng.Fori(0, turns) as i:
            for u in range(STACK):
                step(Batch(i, full_from + u, count))
    for b in range(full_from + turns * STACK, count + 2):
        step(Batch(0, b, count))


def build(nc, hidden, Wq, Wk_down, Wv_down, q_to_latent, v_up, Wout, w_gate, w1, w3, w2, out):
    B, T, E = hidden.shape
    H, D, L = q_to_latent.shape
    TT = T // P
    QUAD = 4
    QUADS = H // QUAD
    HP = QUAD // 2
    EB = 10
    MB = EB // 2
    CT = 32
    SC = float(L) ** -0.5
    X = w_gate.shape[1]
    TOP = 2
    F = w1.shape[2]
    FC = F // P
    TOKENS = B * T
    REGION = TOKENS + P
    ROW = E + 2
    SPARE = X * REGION
    JOBS = -(-(TOP * TOKENS + X * (P - 1)) // P)
    JOBS += JOBS % 2
    NOWHERE = float(4 * TOKENS)

    xs_dram = nc.dram_tensor("expert_rows", (SPARE + P, ROW), FP32, kind="Internal").ap()
    y_dram = nc.dram_tensor("expert_results", (TOP * TOKENS, E), FP32, kind="Internal").ap()
    x1_dram = nc.dram_tensor("x1", (TOKENS, E), FP32, kind="Internal").ap()

    keep = ExitStack()
    base = keep.enter_context(nc.sbuf_tensor("next_row", [P, X], FP32))
    ident = keep.enter_context(nc.sbuf_tensor("ident", [P, P], FP32))
    eps_col = keep.enter_context(nc.sbuf_tensor("eps_col", [P, 1], FP32))
    region0 = keep.enter_context(nc.sbuf_tensor("region0", [P, X], FP32))
    job_x = keep.enter_context(nc.sbuf_tensor("job_x", [1, JOBS], INT32))
    job_row = keep.enter_context(nc.sbuf_tensor("job_row", [1, JOBS], INT32))
    probs = keep.enter_context(nc.sbuf_tensor("probs", [P, 2, EB, T], FP32))
    w13 = probs[:, 0].rearrange("p k t -> p (k t)")[:, 0:X * 2 * F].rearrange("p (x f) -> p x f", x=X)
    w2s = probs[:, 1].rearrange("p k t -> p (k t)")[:, 0:F * X * E // P].rearrange("p (x c e) -> p x c e", x=X, e=E)

    ctx = ExitStack()
    with ctx:
        def sb(name, shape, dt=FP32):
            return ctx.enter_context(nc.sbuf_tensor(name, shape, dt))

        def ps(name, shape, dt=FP32):
            return ctx.enter_context(nc.psum_tensor(name, shape, dt))

        def sem(name):
            return ctx.enter_context(nc.semaphore(name))

        def sems(name, n):
            return [sem(f"{name}{i}") for i in range(n)]

        def dram(name, shape, dt=FP32):
            return nc.dram_tensor(name, shape, dt, kind="Internal").ap()

        parts_dram = [[dram(f"parts_{w}{i}", (PARTS, D, H, T), BF16) for i in range(STACK)] for w in "qk"]
        heads_dram = [dram(f"heads_{i}", (H, D + 1, T)) for i in range(STACK)]
        recip_dram = [dram(f"recip_{i}", (H, T)) for i in range(STACK)]

        ident_bf = sb("ident_bf", [P, P], BF16)
        ahead = sb("ahead", [P, 2, P], BF16)
        wq_nat = sb("wq_nat", [P, E])
        wout_nat = sb("wout_nat", [P, E])
        qtl_nat = sb("qtl_nat", [P, L])
        wkd = sb("wkd", [L, E])
        wvd = sb("wvd", [L, E])
        vup = sb("vup", [L, H, D])
        qtlT = sb("qtlT", [L, P])
        wqT = sb("wqT", [P, H * D])
        wkT = sb("wkT", [P, H * D])
        wvT = sb("wvT", [P, H * D])
        woutT = sb("woutT", [P, E])
        x_in = sb("x_in", [P, STACK, TT, E])
        x_res = sb("x_res", [P, STACK, TT, E])
        xT = sb("xT", [P, T])
        qk_parts = [sb("q_parts", [P, PARTS, T], BF16), sb("k_parts", [P, PARTS, T], BF16)]
        qk_rest = [sb("q_rest", [P, T]), sb("k_rest", [P, T])]
        q_stack = [sb(f"q_stack{i}", [P, H, T], BF16) for i in range(STACK)]
        k_stack = [sb(f"k_stack{i}", [P, H, T], BF16) for i in range(STACK)]
        v_aug = sb("v_aug", [P, STACK, TT * H * 2 * D + CT - 2 * D])
        part_max = sb("part_max", [P, QUADS * HP, 5, 4])
        row_max = sb("row_max", [P, H, TT])
        max_parts = sb("max_parts", [H * TT, PARTS, P], BF16)
        max_rest = sb("max_rest", [H * TT, P])
        heads_out = sb("heads_out", [P, QUADS, T])
        numer = sb("numer", [P, T])
        denom = sb("denom", [P, T * H // P])
        rden = sb("rden", [P, T * H // P])
        rden_all = sb("rden_all", [P, T])
        headsT = sb("headsT", [P, T])
        stats = sb("stats", [P, TT, 6])
        mean_var = sb("mean_var", [P, TT, 2])
        log_var = sb("log_var", [P, TT])
        rstd = sb("rstd", [P, TT])
        image = sb("image", [P, TT, TOP, ROW])
        x1T = xT
        wg = sb("wg", [E, X])
        before = sb("before", [P, P], BF16)
        ones_bf = sb("ones_bf", [P, P], BF16)
        tmp_f = sb("tmp_f", [P, P])
        iota_i = sb("iota_i", [P, X], INT32)
        iota_x = sb("iota_x", [P, X])
        dest_i = sb("dest_i", [P, TT * TOP], INT32)
        dest = sb("dest", [P, TT, TOP])
        logits = sb("logits", [P, TT, X])
        top = sb("top", [P, TT, 8])
        top_at = sb("top_at", [P, TT, 8], UINT32)
        top_f = sb("top_f", [P, TT, TOP])
        chosen_bf = sb("chosen_bf", [P, TT, TOP, X], BF16)
        gap = sb("gap", [P, TT])
        odds = sb("odds", [P, TT])
        odds1 = sb("odds1", [P, TT])
        row_of = sb("row_of", [P, TT, X])
        picked = sb("picked", [P, TT, TOP, X])
        row_f = sb("row_f", [P, TT, TOP])
        row_i = sb("row_i", [P, TT, TOP], UINT32)
        iota_ji = sb("iota_ji", [1, JOBS], INT32)
        iota_j = sb("iota_j", [1, JOBS])
        rows_n = sb("rows_n", [P, X])
        tiles_i = sb("tiles_i", [P, X], INT32)
        tiles = sb("tiles", [P, X])
        ones_x = sb("ones_x", [P, X])
        tile_end = sb("tile_end", [P, X])
        tile_start = sb("tile_start", [P, X])
        lead = sb("lead", [P, X])
        job_xf = sb("job_xf", [1, JOBS])
        job_rf = sb("job_rf", [1, JOBS])
        job_sf = sb("job_sf", [1, JOBS])
        pad_i = sb("pad_i", [P, X], INT32)
        padding = sb("padding", [P, ROW])
        values_flat = v_aug[0:1].rearrange("p s n -> p (s n)")
        probs_flat = probs[0:1, 1].rearrange("p k t -> p (k t)")
        past_end, inside, first = [a.rearrange("p (j x) -> p j x", x=X) for a in (
            values_flat[:, 0:JOBS * X], values_flat[:, JOBS * X:2 * JOBS * X], probs_flat[:, EB * T - JOBS * X:EB * T])]

        score = ps("score", [P, 2, T])
        maxs = ps("maxs", [P, 2, 2, T])
        attn = ps("attn", [P, T])
        misc = ps("misc", [P, T])

        s_passed_pool, s_passed_dve, s_passed_pe = sem("pool_passed"), sem("dve_passed"), sem("pe_passed")
        s_w = sem("weights_loaded")
        s_const = sem("constants_made")
        s_wt = sem("weight_product_done")
        s_wc = sem("weight_copied")
        s_zero = sems("stacks_cleared", STACK)
        s_vones = sem("v_ones_made")
        s_xin = sems("x_in_loaded", STACK)
        s_xres = sems("x_res_loaded", STACK)
        s_xt = sem("x_transposed")
        s_xtc = sem("xT_copied")
        s_proj = sem("q_or_k_projected")
        s_hi = sem("part0_made")
        s_mid = sem("part1_made")
        s_rest = sem("rest_made")
        s_parts = sem("parts_made")
        s_pst = [sems("q_parts_stored", STACK), sems("k_parts_stored", STACK)]
        s_stk = sems("stack_loaded", STACK)
        s_v = sem("v_projected")
        s_vc = sem("v_copied")
        s_msc = sem("scores_for_max_ready")
        s_mx = sem("block_maxima_taken")
        s_rm = sem("row_max_combined")
        s_nmt = sem("row_max_transposed")
        s_nm0 = sem("max_part0_made")
        s_nmr = sem("max_rest_made")
        s_nm1 = sem("max_part1_made")
        s_nmp = sem("max_parts_made")
        s_nmd = sems("max_rows_loaded", STACK)
        s_sc = sem("scores_ready")
        s_exp = sem("exp_done")
        s_tri = sem("future_cleared")
        s_pv = sem("quad_attended")
        s_oc = sem("quad_copied")
        s_hd = sems("heads_stored", STACK)
        s_nd = sems("numer_denom_loaded", STACK)
        s_rd = sem("recip_made")
        s_rst = sems("recip_stored", STACK)
        s_rl = sems("recip_loaded", STACK)
        s_ht = sem("heads_normalized")
        s_op = sem("out_projected")
        s_res = sem("residual_added")
        s_st = sem("stats_step")
        s_ln = sem("log_made")
        s_rs = sem("rstd_made")
        s_x1 = sem("x1_made")
        s_out = sem("x1_stored")
        s_x1t = sem("x1_transposed")
        s_x1tc = sem("x1T_copied")
        s_lg = sem("logits_ready")
        s_ch = sem("choice_step")
        s_oh = sem("choice_made")
        s_gap = sem("gap_made")
        s_odds = sem("odds_made")
        s_rk = sem("ranks_ready")
        s_rr = sem("ranks_read")
        s_ro = sem("row_step")
        s_im = sem("image_doubled")
        s_rows = sem("rows_made")
        s_sct = sem("rows_scattered")
        s_pl = sem("plan_step")
        s_padi = sem("padding_rows_known")
        s_pad = sem("padding_stored")
        s_ew = sem("expert_weights_loaded")

        WEIGHTS = 8 * 16
        def exps(b, g, k):
            return (b.num * QUADS + g) * EB + k + 1
        def maxes(b, g, k):
            return (b.num * QUADS + g) * MB + k + 1
        TRI = 6
        def quad(b, g):
            return b.num * QUADS + g
        NX = STACK

        x_dram = hidden.rearrange("b (i p) e -> b p i e", p=P)
        x1_v = x1_dram.rearrange("(b i p) e -> b p i e", p=P, i=TT)


        def clear_stacks(eng, i):
            for n, stack in enumerate((q_stack[i], k_stack[i])):
                eng.memset(stack[:].rearrange("p h t -> p (h t)").bitcast(FP32), 0.0).then_inc(s_zero[i], 1)
            eng.wait_ge(s_zero[i], 2)
            eng.memset(k_stack[i][MAX_ROW:P], 1.0).then_inc(s_zero[i], 1)
            eng.wait_ge(s_zero[i], 3)

        block = ctx.enter_context(nc.Block())

        @block.sync
        def _(sp):
            sp.dma_start(wq_nat[:], Wq).then_inc(s_w, 16)
            sp.dma_start(wout_nat[:], Wout).then_inc(s_w, 16)
            sp.dma_start(qtl_nat[:], q_to_latent.rearrange("h d l -> (h d) l")).then_inc(s_w, 16)
            sp.dma_start(wkd[:], Wk_down).then_inc(s_w, 16)
            sp.dma_start(wg[:], w_gate).then_inc(s_w, 16)
            sp.dma_start(wvd[:], Wv_down).then_inc(s_w, 16)
            sp.dma_start(vup[:, 0:H // 2], v_up[0:H // 2].rearrange("h l d -> l h d")).then_inc(s_w, 16)
            sp.dma_start(vup[:, H // 2:H], v_up[H // 2:H].rearrange("h l d -> l h d")).then_inc(s_w, 16)

            def store_parts(b, w):
                sp.wait_ge(s_parts, 2 * b.num + w + 1)
                for p in range(PARTS):
                    sp.dma_start(parts_dram[w][b.buf][p].rearrange("d h t -> h d t"), qk_parts[w][:, p, :])\
                      .then_inc(s_pst[w][b.buf], 16)

            def load_stack(b, w):
                parts, rows, stack = parts_dram[w][b.buf], (Q_ROWS, K_ROWS)[w], (q_stack, k_stack)[w][b.buf]
                sp.wait_ge(s_pst[w][b.buf], PARTS * 16 * (b.round + 1))
                sp.wait_ge(s_zero[b.buf], 3)
                wait(sp, s_sc, exps(b.plus(-STACK), QUADS - 1, EB - 1))
                for first, part, n in rows:
                    dst = stack[first * D:(first + n) * D].rearrange("p h t -> p (h t)")
                    if w == 0:
                        src = parts[part:part + 1].rearrange("o d h t -> o d (h t)").broadcast_to([n, D, H * T])
                    else:
                        src = parts[part:part + n].rearrange("o d h t -> (o d) (h t)")
                    sp.dma_start(dst, src).then_inc(s_stk[b.buf], 16)

            def step(b):
                done, prev, nxt, far = b.plus(-2), b.plus(-1), b.plus(1), b.plus(2)
                if far.exists:
                    wait(sp, s_xt, far.num - STACK + 1)
                    sp.dma_start(x_in[:, far.buf], x_dram[far.num]).then_inc(s_xin[far.buf], 16)
                if prev.exists:
                    sp.dma_start(x_res[:, prev.buf], x_dram[prev.num]).then_inc(s_xres[prev.buf], 16)
                if done.exists:
                    sp.wait_ge(s_x1, done.num + 1)
                    sp.dma_start(x1_v[done.num], image[:, :, 0, 0:E]).then_inc(s_out, 16)
                if far.exists:
                    store_parts(far, 0)
                if prev.exists:
                    sp.wait_ge(s_oc, quad(prev, QUADS - 1) + 1)
                    dst = heads_dram[prev.buf].rearrange("(g q) r t -> q r g t", q=QUAD)
                    for q in range(QUAD):
                        sp.dma_start(dst[q], heads_out[CT * q:CT * q + D + 1]).then_inc(s_hd[prev.buf], 16)
                if far.exists:
                    load_stack(far, 0)
                if prev.exists:
                    sp.wait_ge(s_hd[prev.buf], QUAD * 16 * (prev.round + 1))
                    wait(sp, s_ht, prev.num)
                    sp.dma_start(denom[:], heads_dram[prev.buf][:, D, :].rearrange("h (c t) -> h c t", c=D))\
                      .then_inc(s_nd[prev.buf], 16)
                    sp.dma_start(numer[:], heads_dram[prev.buf][:, 0:D, :]).then_inc(s_nd[prev.buf], 16)
                if far.exists:
                    store_parts(far, 1)
                    load_stack(far, 1)
                if prev.exists:
                    sp.wait_ge(s_rd, prev.num + 1)
                    sp.dma_start(recip_dram[prev.buf].rearrange("h (c t) -> h c t", c=D), rden[:])\
                      .then_inc(s_rst[prev.buf], 16)
                    sp.wait_ge(s_rst[prev.buf], 16 * (prev.round + 1))
                    sp.dma_start(rden_all[:],
                                 recip_dram[prev.buf].rearrange("h (o t) -> h o t", o=1).broadcast_to([H, D, T]))\
                      .then_inc(s_rl[prev.buf], 16)
                if nxt.exists:
                    sp.wait_ge(s_nmp, nxt.num + 1)
                    for p in range(PARTS):
                        sp.dma_start(q_stack[nxt.buf][MAX_ROW + p:MAX_ROW + p + 1].rearrange("o h (i t) -> o (h i) t", i=TT),
                                     max_parts[:, p, :]).then_inc(s_nmd[nxt.buf], 16)

            over_batches(sp, B, step)
            sp.wait_ge(s_pv, QUADS * B)
            sp.dma_start(w13[:, :, 0:F], w1.rearrange("x e f -> e x f")).then_inc(s_ew, 16)
            sp.dma_start(w13[:, :, F:2 * F], w3.rearrange("x e f -> e x f")).then_inc(s_ew, 16)
            sp.dma_start(w2s.rearrange("p x c e -> p (x c) e"), w2.rearrange("x (c p) e -> p (x c) e", p=P)).then_inc(s_ew, 16)
            sp.wait_ge(s_const, 16)
            sp.dma_start(xs_dram[SPARE:SPARE + P, :], padding[:]).then_inc(s_pad, 16)
            sp.wait_ge(s_padi, 1)
            for x in range(X):
                row = sp.value_load(pad_i[0:1, x:x + 1], min_val=0, max_val=SPARE - P)
                sp.dma_start(xs_dram[bass.ds(row, P), :], padding[:]).then_inc(s_pad, 16)
            sp.wait_ge(s_pad, 16 * (X + 1))
            sp.wait_ge(s_ew, 48)
            sp.wait_ge(s_out, 16 * B)

        @block.gpsimd
        def _(pool):
            pool.memset(ident[:], 0.0).then_inc(s_const, 1)
            pool.memset(ahead[:], 0.0).then_inc(s_const, 1)
            pool.wait_ge(s_const, 2)
            pool.affine_select(out=ident[:], in_=ident[:], compare_op=ALU.not_equal, fill=1.0, base=0,
                               pattern=[[-1, P]], channel_multiplier=1).then_inc(s_const, 1)
            pool.affine_select(out=ahead[:], in_=ahead[:], compare_op=ALU.is_ge, fill=NEG, base=0,
                               pattern=[[0, 2], [-1, P]], channel_multiplier=1).then_inc(s_const, 1)
            pool.wait_ge(s_const, 4)
            pool.tensor_copy(ident_bf[:], ident[:]).then_inc(s_const, 1)
            pool.memset(eps_col[:], EPS).then_inc(s_const, 1)
            pool.memset(ones_bf[:], 1.0).then_inc(s_const, 1)
            pool.memset(tmp_f[:], 1.0).then_inc(s_const, 1)
            pool.iota(iota_i[:], pattern=[[1, X]], base=0, channel_multiplier=0).then_inc(s_const, 1)
            pool.iota(dest_i[:], pattern=[[P, TT], [TOKENS, TOP]], base=0, channel_multiplier=1).then_inc(s_const, 1)
            pool.wait_ge(s_const, 10)
            pool.affine_select(out=tmp_f[:], in_=tmp_f[:], compare_op=ALU.is_gt, fill=0.0, base=0,
                               pattern=[[1, P]], channel_multiplier=-1).then_inc(s_const, 1)
            pool.wait_ge(s_const, 11)
            pool.tensor_copy(before[:], tmp_f[:]).then_inc(s_const, 1)
            pool.iota(iota_ji[:], pattern=[[1, JOBS]], base=0, channel_multiplier=0).then_inc(s_const, 1)
            pool.memset(ones_x[:], 1.0).then_inc(s_const, 1)
            pool.memset(padding[:], 0.0).then_inc(s_const, 1)
            pool.wait_ge(s_const, 15)
            pool.memset(padding[:, E + 1:E + 2], NOWHERE).then_inc(s_const, 1)
            for i in range(STACK):
                pool.memset(v_aug[:, i], 1.0).then_inc(s_vones, 1)
            for i in range(1, STACK):
                clear_stacks(pool, i)

            def step(b):
                prev, far, done = b.plus(-1), b.plus(2), b.plus(-2)

                def clear_future(g, pr):
                    k, pt = 5 * pr, probs[:, g % 2]
                    full = pt[:, k:k + 2, 0:P]
                    wait_apart(pool, s_exp, exps(b, g, k + 1), s_passed_pool)
                    pool.affine_select(out=full, in_=full, compare_op=ALU.is_ge, fill=0.0, base=0,
                                       pattern=[[0, 2], [1, P]], channel_multiplier=-1).then_inc(s_tri, 1)
                    odd = pt[:, k + 2:k + 4, 0:2 * P].rearrange("p e (i t) -> p e i t", i=2)
                    wait_apart(pool, s_exp, exps(b, g, k + 3), s_passed_pool)
                    pool.affine_select(out=odd, in_=odd, compare_op=ALU.is_ge, fill=0.0, base=0,
                                       pattern=[[0, 2], [0, 2], [1, P]], channel_multiplier=-1).then_inc(s_tri, 1)
                    both = pt[:, k + 4, :].rearrange("p (e t) -> p e t", e=2)[:, :, 0:P]
                    wait_apart(pool, s_exp, exps(b, g, k + 4), s_passed_pool)
                    pool.affine_select(out=both, in_=both, compare_op=ALU.is_ge, fill=0.0, base=0,
                                       pattern=[[0, 2], [1, P]], channel_multiplier=-1).then_inc(s_tri, 1)

                def last_part(w):
                    wait_apart(pool, s_mid, 2 * far.num + w + 1, s_passed_pool)
                    pool.tensor_tensor(qk_parts[w][:, 2, :], qk_rest[w][:], qk_parts[w][:, 1, :], ALU.subtract)\
                        .then_inc(s_parts, 1)

                def scatter(tiles):
                    wait_apart(pool, s_rows, done.num + 1, s_passed_pool)
                    wait_apart(pool, s_im, done.num + 1, s_passed_pool)
                    for i in tiles:
                        for j in range(TOP):
                            pool.indirect_dma_start(
                                out=xs_dram, out_offset=bass.IndirectOffsetOnAxis(ap=row_i[:, i, j:j + 1], axis=0),
                                in_=image[:, i, j, :], in_offset=None).then_inc(s_sct, 16)

                for g in range(QUADS):
                    for pr in range(HP):
                        if b.exists:
                            clear_future(g, pr)
                        if (g, pr) in ((0, 1), (1, 0)) and far.exists:
                            last_part(g)
                        if (g, pr) == (1, 1) and done.exists:
                            wait_apart(pool, s_x1, done.num + 1, s_passed_pool)
                            pool.tensor_copy(image[:, :, 1, 0:E], image[:, :, 0, 0:E]).then_inc(s_im, 1)
                        if (g, pr) == (2, 1) and prev.exists:
                            wait_apart(pool, s_rl[prev.buf], 16 * (prev.round + 1), s_passed_pool)
                            wait_apart(pool, s_nd[prev.buf], 2 * 16 * (prev.round + 1), s_passed_pool)
                            wait_apart(pool, s_op, prev.num, s_passed_pool)
                            pool.tensor_tensor(headsT[:], numer[:], rden_all[:], ALU.mult).then_inc(s_ht, 1)
                        if g == 3 and done.exists:
                            scatter(range(TT // HP * pr, TT // HP * (pr + 1)))

            over_batches(pool, B, step)
            pool.wait_ge(s_sct, TT * TOP * 16 * B)

        @block.tensor
        def _(pe):
            pe.wait_ge(s_w, WEIGHTS)
            pe.wait_ge(s_const, 3)
            pe.transpose(misc[:, 0:P], wq_nat[:], ident[:]).then_inc(s_wt, 1)
            pe.transpose(misc[:, P:2 * P], wout_nat[:], ident[:]).then_inc(s_wt, 1)
            pe.transpose(misc[0:L, 2 * P:3 * P], qtl_nat[:], ident[:]).then_inc(s_wt, 1)
            pe.wait_ge(s_wc, 3)
            pe.matmul(misc[:, 0:P], wkd[:], qtlT[:], start=True, stop=True).then_inc(s_wt, 1)
            pe.matmul(misc[:, P:2 * P], wvd[:], vup[:].rearrange("l h d -> l (h d)"), start=True, stop=True)\
              .then_inc(s_wt, 1)
            pe.wait_ge(s_wc, 5)

            pe.wait_ge(s_wc, 5)

            def score_unit(b, g, k):
                n = exps(b, g, k)
                if k == 0 and g == 0:
                    pe.wait_ge(s_nmd[b.buf], PARTS * 16 * (b.round + 1))
                wait(pe, s_exp, n - 2)
                bank, kk, pr = score[:, k % 2], k % 5, k // 5
                ks, qs = k_stack[b.buf], q_stack[b.buf]
                R = MAX_ROW + PARTS

                def mm(c0, j, h, start):
                    return pe.matmul(bank[:, c0:c0 + T - P * j], ks[0:R, h, P * j:P * j + P], qs[0:R, h, P * j:T],
                                     start=start, stop=True, skip_group_check=True)
                h0 = QUAD * g + 2 * pr
                if kk < 2:
                    last = mm(0, 0, h0 + kk, True)
                elif kk < 4:
                    mm(0, 3, h0 + kk - 2, True)
                    last = mm(P, 1, h0 + kk - 2, False)
                else:
                    mm(0, 2, h0, True)
                    last = mm(2 * P, 2, h0 + 1, False)
                last.then_inc(s_sc, 1)

            def max_bank(b, g, k):
                n = maxes(b, g, k // 2)
                if k == 0 and g == 0:
                    pe.wait_ge(s_stk[b.buf], 6 * 16 * (b.round + 1))
                if k % 2 == 0:
                    wait(pe, s_mx, n - 2)
                bank, kk, pr = maxs[:, (g * MB + k // 2) % 2, k % 2], k % 5, k // 5
                ks, qs = k_stack[b.buf], q_stack[b.buf]

                def mm(c0, i, h, start):
                    pe.matmul(bank[:, c0:c0 + P * (i + 1)], qs[0:MAX_ROW, h, P * i:P * i + P],
                              ks[0:MAX_ROW, h, 0:P * (i + 1)], start=start, stop=False, skip_group_check=True)

                def mask(cols, n):
                    return pe.matmul(cols, ident_bf[:], ahead[:, 0:n], start=False, stop=True, skip_group_check=True)
                h0 = QUAD * g + 2 * pr
                if kk < 2:
                    mm(0, 3, h0 + kk, True)
                    last = mask(bank[:, 3 * P:4 * P], 1)
                elif kk < 4:
                    mm(0, 2, h0 + kk - 2, True)
                    mm(3 * P, 0, h0 + kk - 2, False)
                    last = mask(bank[:, 2 * P:4 * P], 2)
                else:
                    mm(0, 1, h0, True)
                    mm(2 * P, 1, h0 + 1, False)
                    last = mask(bank.rearrange("p (e t) -> p e t", e=2)[:, :, P:2 * P], 2)
                if k % 2:
                    last.then_inc(s_msc, 1)

            def attend(b, g, j):
                if j == 0:
                    pe.wait_ge(s_tri, TRI * (quad(b, g) + 1))
                    wait(pe, s_oc, quad(b, g))
                    if g == 0:
                        pe.wait_ge(s_vc, b.num + 1)
                pt = probs[:, g % 2]
                for q in range(QUAD):
                    v0 = (j * H + QUAD * g + q) * 2 * D
                    pr, e = q // 2, q % 2
                    if j == 0:
                        src = pt[:, 5 * pr + e, :]
                    elif j == 1:
                        src = pt[:, 5 * pr + 2 + e, P:T]
                    elif j == 2:
                        src = pt[:, 5 * pr + 4, 2 * P * e:2 * P * (e + 1)]
                    else:
                        src = pt[:, 5 * pr + 2 + e, 0:P]
                    last = pe.matmul(attn[CT * q:CT * (q + 1), P * j:T], v_aug[:, b.buf, v0:v0 + CT], src,
                                     start=j == 0, stop=j == TT - 1)
                if j == TT - 1:
                    last.then_inc(s_pv, 1)

            def small(b, g, k):
                prev, nxt, far = b.plus(-1), b.plus(1), b.plus(2)
                done = b.plus(-2)
                if (g, k) == (0, 0) and far.exists:
                    pe.wait_ge(s_xin[far.buf], 16 * (far.round + 1))
                    wait(pe, s_vc, far.num)
                    wait(pe, s_nmr, b.num + 1)
                    wait(pe, s_rr, done.num)
                    wait(pe, s_res, done.num + 1)
                    for i in range(TT):
                        last = pe.transpose(misc[:, P * i:P * i + P], x_in[:, far.buf, i, :], ident[:])
                    last.then_inc(s_xt, 1)
                if (g, k) in ((0, 3), (0, 7)) and far.exists:
                    w = int(k == 7)
                    if w == 0:
                        pe.wait_ge(s_xtc, far.num + 1)
                    else:
                        pe.wait_ge(s_rest, 2 * far.num + w)
                    pe.matmul(misc[:], (wqT, wkT)[w][:], xT[:], start=True, stop=True).then_inc(s_proj, 1)
                if (g, k) == (1, 1) and far.exists:
                    pe.wait_ge(s_rest, 2 * far.num + 2)
                    for i in range(TT):
                        last = pe.matmul(misc[:, P * i:P * i + P], xT[:, P * i:P * i + P], wvT[:], start=True, stop=True)
                    last.then_inc(s_v, 1)
                if (g, k) == (1, 5) and done.exists:
                    pe.wait_ge(s_x1, done.num + 1)
                    if far.exists:
                        pe.wait_ge(s_vc, far.num + 1)
                    wait(pe, s_res, done.num + 1)
                    for i in range(TT):
                        last = pe.transpose(misc[:, P * i:P * i + P], image[:, i, 0, 0:E], ident[:])
                    last.then_inc(s_x1t, 1)
                if (g, k) == (1, 9) and done.exists:
                    pe.wait_ge(s_x1tc, done.num + 1)
                    for i in range(TT):
                        last = pe.matmul(misc[:, X * i:X * i + X], x1T[:, P * i:P * i + P], wg[:], start=True, stop=True)
                    last.then_inc(s_lg, 1)
                if (g, k) == (2, 7) and done.exists:
                    pe.wait_ge(s_oh, done.num + 1)
                    n = 0
                    for j in range(TOP):
                        ch = chosen_bf[:, :, j, :]
                        pe.matmul(misc[:, 0:TT * X].rearrange("p (i x) -> p i x", i=TT), before[:], ch, start=j == 0, stop=False,
                                  skip_group_check=True)
                        for s in range(1, TT):
                            pe.matmul(misc[:, s * X:TT * X].rearrange("p (i x) -> p i x", x=X), ones_bf[:], ch[:, 0:TT - s],
                                      start=False, stop=False, skip_group_check=True)
                        for i in range(TT):
                            last = pe.matmul(misc[:, TT * X:TT * X + X], ones_bf[:], ch[:, i], start=False, stop=True,
                                             skip_group_check=True)
                    last.then_inc(s_rk, 1)
                if (g, k) == (3, 2) and nxt.exists:
                    pe.wait_ge(s_rm, nxt.num + 1)
                    if far.exists:
                        pe.wait_ge(s_vc, far.num + 1)
                    wait(pe, s_rr, done.num + 1)
                    wait_apart(pe, s_res, prev.num, s_passed_pe)
                    pe.transpose(misc[0:H * TT, 0:P], row_max[:].rearrange("p h i -> p (h i)"), ident[:]).then_inc(s_nmt, 1)
                if (g, k) == (3, 6) and prev.exists:
                    if nxt.exists:
                        pe.wait_ge(s_nmr, nxt.num + 1)
                    wait(pe, s_rr, done.num + 1)
                    wait(pe, s_res, prev.num)
                    pe.wait_ge(s_ht, prev.num + 1)
                    for i in range(TT):
                        last = pe.matmul(misc[:, P * i:P * i + P], headsT[:, P * i:P * i + P], woutT[:], start=True, stop=True)
                    last.then_inc(s_op, 1)

            def step(b):
                for g in range(QUADS):
                    mb, mg = (b.plus(1), g + 1) if g + 1 < QUADS else (b.plus(2), 0)
                    pb, pg = (b, g - 1) if g else (b.plus(-1), QUADS - 1)
                    for k in range(EB):
                        if b.exists:
                            score_unit(b, g, k)
                        small(b, g, k)
                        if mb.exists:
                            max_bank(mb, mg, k)
                        if pb.exists and k % 2 and k > 1:
                            attend(pb, pg, k // 2 - 1)

            over_batches(pe, B, step)

        @block.scalar
        def _(act):
            act.preload_act_table_set("natural_log_exp_and_others")

            def step(b):
                prev, nxt, far, done = b.plus(-1), b.plus(1), b.plus(2), b.plus(-2)
                for g in range(QUADS):
                    ob, og = (b, g - 2) if g >= 2 else (b.plus(-1), g + QUADS - 2)
                    for k in range(EB):
                        if b.exists:
                            if k == 0:
                                wait(act, s_pv, quad(b, g) - 1)
                            act.wait_ge(s_sc, exps(b, g, k))
                            act.activation(probs[:, g % 2, k, :], score[:, k % 2], ACT.Exp).then_inc(s_exp, 1)
                        if (g, k) == (0, 1) and far.exists:
                            act.wait_ge(s_xt, far.num + 1)
                            wait(act, s_v, far.num)
                            act.activation(xT[:], misc[:], ACT.Copy).then_inc(s_xtc, 1)
                        if (g, k) in ((0, 7), (1, 1)) and far.exists:
                            w = g
                            act.wait_ge(s_rest, 2 * far.num + w + 1)
                            act.activation(qk_parts[w][:, 1, :], qk_rest[w][:], ACT.Copy).then_inc(s_mid, 1)
                        if (g, k) in ((0, 4), (0, 8)) and far.exists:
                            w = int(k == 8)
                            act.wait_ge(s_proj, 2 * far.num + w + 1)
                            before = far.plus(-1)
                            wait(act, s_pst[w][before.buf], PARTS * 16 * (before.round + 1))
                            act.activation(qk_parts[w][:, 0, :], misc[:], ACT.Copy).then_inc(s_hi, 1)
                        if ob.exists and k == 1 and og % 2 == 0:
                            act.wait_ge(s_pv, quad(ob, og) + 1)
                            if og == 0:
                                before = ob.plus(-1)
                                wait(act, s_hd[before.buf], QUAD * 16 * (before.round + 1))
                            act.activation(heads_out[:, og], attn[:], ACT.Copy).then_inc(s_oc, 1)
                        if (g, k) == (3, 3) and nxt.exists:
                            act.wait_ge(s_nmt, nxt.num + 1)
                            wait(act, s_nmd[b.buf], PARTS * 16 * (b.round + 1))
                            act.activation(max_parts[:, 0, :], misc[0:H * TT, 0:P], ACT.Copy, scale=-1.0).then_inc(s_nm0, 1)
                        if (g, k) == (1, 6) and done.exists:
                            act.wait_ge(s_x1t, done.num + 1)
                            act.activation(x1T[:], misc[:], ACT.Copy).then_inc(s_x1tc, 1)
                        if (g, k) == (2, 6) and done.exists:
                            act.wait_ge(s_gap, done.num + 1)
                            act.activation(odds[:], gap[:], ACT.Exp).then_inc(s_odds, 1)
                        if (g, k) == (0, 2) and done.exists:
                            act.wait_ge(s_st, 2 * (done.num + 1))
                            act.activation(log_var[:], mean_var[:, :, 1], ACT.Ln, bias=eps_col[:]).then_inc(s_ln, 1)
                            act.wait_ge(s_ln, done.num + 1)
                            act.activation(rstd[:], log_var[:], ACT.Exp, scale=-0.5).then_inc(s_rs, 1)

            act.wait_ge(s_const, 6)
            over_batches(act, B, step)

        @block.vector
        def _(dve):
            clear_stacks(dve, 0)
            for n, (dst, src, scale) in enumerate([
                (wqT[:], misc[:, 0:P], SC), (woutT[:], misc[:, P:2 * P], 1.0), (qtlT[:], misc[0:L, 2 * P:3 * P], 1.0),
                (wkT[:], misc[:, 0:P], 1.0), (wvT[:], misc[:, P:2 * P], 1.0),
            ]):
                dve.wait_ge(s_wt, 3 if n < 3 else 5)
                dve.tensor_scalar_mul(dst, src, scale).then_inc(s_wc, 1)

            dve.wait_ge(s_const, 12)
            dve.tensor_copy(iota_x[:], iota_i[:]).then_inc(s_ch, 1)
            dve.tensor_copy(dest[:].rearrange("p i j -> p (i j)"), dest_i[:]).then_inc(s_ch, 1)
            dve.wait_ge(s_ch, 2)
            dve.tensor_scalar_mul(region0[:], iota_x[:], float(REGION)).then_inc(s_ch, 1)
            dve.tensor_scalar_mul(base[:], iota_x[:], float(REGION)).then_inc(s_ch, 1)
            CHOICE, PLACE = 4, 8

            def choose(b):
                n = 4 + CHOICE * b.num
                dve.wait_ge(s_lg, b.num + 1)
                dve.tensor_copy(logits[:].rearrange("p i x -> p (i x)"), misc[:, 0:TT * X]).then_inc(s_ch, 1)
                wait_apart(dve, s_ch, n + 1, s_passed_dve)
                for i in range(TT):
                    last = dve.max(top[:, i], logits[:, i])
                last.then_inc(s_ch, 1)
                dve.wait_ge(s_ch, n + 2)
                dve.tensor_tensor(gap[:], top[:, :, 1], top[:, :, 0], ALU.subtract).then_inc(s_gap, 1)
                for i in range(TT):
                    last = dve.max_index(top_at[:, i], top[:, i], logits[:, i])
                last.then_inc(s_ch, 1)
                dve.wait_ge(s_ch, n + 3)
                dve.tensor_copy(top_f[:], top_at[:, :, 0:TOP]).then_inc(s_ch, 1)
                dve.wait_ge(s_ch, n + 4)
                dve.tensor_tensor(chosen_bf[:].rearrange("p i j x -> p (i j) x"),
                                  iota_x[:].rearrange("p (o x) -> p o x", o=1).to_broadcast([P, TT * TOP, X]),
                                  top_f[:].rearrange("p i (j o) -> p (i j) o", o=1).to_broadcast([P, TT * TOP, X]),
                                  ALU.is_equal).then_inc(s_oh, 1)

            def place(b):
                n = PLACE * b.num
                dve.wait_ge(s_rk, b.num + 1)
                dve.tensor_tensor(row_of[:], misc[:, 0:TT * X].rearrange("p (i x) -> p i x", x=X),
                                  base[:].rearrange("p (o x) -> p o x", o=1).to_broadcast([P, TT, X]), ALU.add).then_inc(s_ro, 1)
                dve.wait_ge(s_ro, n + 1)
                dve.tensor_tensor(base[:], base[:], misc[:, TT * X:TT * X + X], ALU.add).then_inc(s_rr, 1)
                for j in range(TOP):
                    last = dve.tensor_tensor(picked[:, :, j], row_of[:], chosen_bf[:, :, j], ALU.mult)
                last.then_inc(s_ro, 1)
                dve.wait_ge(s_ro, n + 2)
                dve.tensor_reduce(row_f[:].rearrange("p i j -> p (i j)"), picked[:].rearrange("p i j x -> p (i j) x"),
                                  AX.X, ALU.add).then_inc(s_ro, 1)
                dve.wait_ge(s_odds, b.num + 1)
                dve.tensor_scalar_add(odds1[:], odds[:], 1.0).then_inc(s_ro, 1)
                dve.wait_ge(s_ro, n + 4)
                dve.reciprocal(image[:, :, 0, E], odds1[:]).then_inc(s_ro, 1)
                dve.wait_ge(s_ro, n + 5)
                dve.tensor_tensor(image[:, :, 1, E], odds[:], image[:, :, 0, E], ALU.mult).then_inc(s_ro, 1)
                dve.tensor_copy(image[:, :, :, E + 1], dest[:]).then_inc(s_ro, 1)
                dve.wait_ge(s_ro, n + 7)
                dve.tensor_scalar_add(dest[:], dest[:], float(T)).then_inc(s_ro, 1)
                dve.wait_ge(s_ro, n + 8)
                dve.tensor_copy(row_i[:], row_f[:]).then_inc(s_rows, 1)

            def max_unit(b, g, m):
                dve.wait_ge(s_msc, maxes(b, g, m))
                flat = part_max[:].rearrange("p a k i -> p (a k i)")
                first = (g * MB + m) * 8
                if m == 0 and g == 0:
                    wait(dve, s_rm, b.num)
                dve.tensor_reduce(flat[:, first:first + 8],
                                  maxs[:, (g * MB + m) % 2].rearrange("p c (i t) -> p (c i) t", t=P), AX.X, ALU.max)\
                   .then_inc(s_mx, 1)

            def step(b):
                prev, nxt, far, done = b.plus(-1), b.plus(1), b.plus(2), b.plus(-2)
                for g in range(QUADS):
                    mb, mg = (b.plus(1), g + 1) if g + 1 < QUADS else (b.plus(2), 0)
                    ob, og = (b, g - 2) if g >= 2 else (b.plus(-1), g + QUADS - 2)
                    for m in range(MB):
                        if mb.exists:
                            max_unit(mb, mg, m)
                        if ob.exists and m == 0 and og % 2 == 1:
                            dve.wait_ge(s_pv, quad(ob, og) + 1)
                            dve.tensor_copy(heads_out[:, og], attn[:]).then_inc(s_oc, 1)
                        if (g, m) in ((0, 2), (0, 4)) and far.exists:
                            w = int(m == 4)
                            dve.wait_ge(s_hi, 2 * far.num + w + 1)
                            dve.tensor_tensor(qk_rest[w][:], misc[:], qk_parts[w][:, 0, :], ALU.subtract).then_inc(s_rest, 1)
                        if (g, m) == (1, 1) and far.exists:
                            dve.wait_ge(s_v, far.num + 1)
                            dve.wait_ge(s_vones, far.buf + 1)
                            wait(dve, s_pv, quad(far.plus(-STACK), QUADS - 1) + 1)
                            v_rows = v_aug[:, far.buf, 0:TT * H * 2 * D].rearrange("p (n d) -> p n d", d=2 * D)
                            dve.tensor_copy(v_rows[:, :, 0:D], misc[:].rearrange("p (n d) -> p n d", d=D))\
                               .then_inc(s_vc, 1)
                        if (g, m) == (2, 1) and done.exists:
                            choose(done)
                        if (g, m) == (2, 4) and done.exists:
                            place(done)
                        if (g, m) == (1, 4) and prev.exists:
                            dve.wait_ge(s_nd[prev.buf], 2 * 16 * (prev.round + 1))
                            dve.reciprocal(rden[:], denom[:]).then_inc(s_rd, 1)
                        if (g, m) == (3, 4) and prev.exists:
                            dve.wait_ge(s_op, prev.num + 1)
                            dve.wait_ge(s_xres[prev.buf], 16 * (prev.round + 1))
                            resid = x_res[:, prev.buf]
                            dve.tensor_tensor(resid.rearrange("p i e -> p (i e)"), misc[:],
                                              resid.rearrange("p i e -> p (i e)"), ALU.add).then_inc(s_res, 1)
                            dve.wait_ge(s_res, prev.num + 1)
                            for i in range(TT):
                                last = dve.bn_stats(stats[:, i], resid[:, i])
                            last.then_inc(s_st, 1)
                            wait_apart(dve, s_st, 2 * prev.num + 1, s_passed_dve)
                            for i in range(TT):
                                last = dve.bn_aggr(mean_var[:, i], stats[:, i])
                            last.then_inc(s_st, 1)
                        if (g, m) == (0, 3) and done.exists:
                            dve.wait_ge(s_rs, done.num + 1)
                            wait(dve, s_out, 16 * done.num)
                            wait(dve, s_sct, TT * TOP * 16 * done.num)
                            for i in range(TT):
                                last = dve.tensor_scalar(image[:, i, 0, 0:E], x_res[:, done.buf, i], mean_var[:, i, 0:1],
                                                         rstd[:, i:i + 1], ALU.subtract, ALU.mult)
                            last.then_inc(s_x1, 1)
                        if (g, m) == (3, 2) and nxt.exists:
                            dve.wait_ge(s_nm0, nxt.num + 1)
                            dve.scalar_tensor_tensor(out=max_rest[:], in0=misc[0:H * TT, 0:P], scalar=-1.0,
                                                     in1=max_parts[:, 0, :], op0=ALU.mult, op1=ALU.subtract).then_inc(s_nmr, 1)
                            dve.wait_ge(s_nmr, nxt.num + 1)
                            dve.tensor_copy(max_parts[:, 1, :], max_rest[:]).then_inc(s_nm1, 1)
                            dve.wait_ge(s_nm1, nxt.num + 1)
                            dve.tensor_tensor(max_parts[:, 2, :], max_rest[:], max_parts[:, 1, :], ALU.subtract)\
                               .then_inc(s_nmp, 1)
                    if g == 2 and nxt.exists:
                        pm = part_max[:]
                        dve.wait_ge(s_mx, maxes(nxt, QUADS - 1, MB - 1))
                        wait(dve, s_nmt, nxt.num)
                        rm = row_max[:].rearrange("p (a e) i -> p a e i", e=2)
                        dve.tensor_reduce(rm[:, :, :, 3], pm[:, :, 0:2, :], AX.X, ALU.max)
                        dve.tensor_reduce(rm[:, :, :, 2], pm[:, :, 2:4, 0:3], AX.X, ALU.max)
                        dve.tensor_reduce(rm[:, :, :, 1], pm[:, :, 4, :].rearrange("p a (e i) -> p a e i", e=2), AX.X, ALU.max)
                        dve.tensor_copy(rm[:, :, :, 0], pm[:, :, 2:4, 3]).then_inc(s_rm, 1)

            over_batches(dve, B, step)

            done = [0]

            def link(ins):
                done[0] += 1
                ins.then_inc(s_pl, 1)
                dve.wait_ge(s_pl, done[0])

            def along(ap):
                return ap.rearrange("p (o x) -> p o x", o=1).to_broadcast([1, JOBS, X])

            def across(ap):
                return ap.rearrange("p (j o) -> p j o", o=1).to_broadcast([1, JOBS, X])

            dve.wait_ge(s_rr, B)
            dve.tensor_copy(pad_i[:], base[:]).then_inc(s_padi, 1)
            link(dve.tensor_copy(iota_j[:], iota_ji[:]))
            link(dve.tensor_tensor(rows_n[:], base[:], region0[:], ALU.subtract))
            link(dve.tensor_scalar_add(rows_n[:], rows_n[:], float(P - 1)))
            link(dve.tensor_copy(tiles_i[:], rows_n[:]))
            link(dve.tensor_single_scalar(tiles_i[:], tiles_i[:], P.bit_length() - 1, ALU.arith_shift_right))
            link(dve.tensor_copy(tiles[:], tiles_i[:]))
            link(dve.tensor_tensor_scan(tile_end[:], ones_x[:], tiles[:], 0.0, ALU.mult, ALU.add))
            link(dve.tensor_tensor(tile_start[:], tile_end[:], tiles[:], ALU.subtract))
            link(dve.tensor_scalar_mul(lead[:], tile_start[:], -float(P)))
            link(dve.tensor_tensor(lead[:], lead[:], region0[:], ALU.add))
            link(dve.tensor_tensor(past_end, across(iota_j[0:1, :]), along(tile_end[0:1, :]), ALU.is_ge))
            link(dve.tensor_tensor(inside, across(iota_j[0:1, :]), along(tile_start[0:1, :]), ALU.is_ge))
            link(dve.tensor_tensor(inside, inside, past_end, ALU.subtract))
            link(dve.tensor_scalar_mul(job_sf[:], iota_j[0:1, :], float(P)))
            link(dve.tensor_tensor(first, across(job_sf[:]), along(lead[0:1, :]), ALU.add))
            link(dve.tensor_tensor(first, first, inside, ALU.mult))
            link(dve.tensor_reduce(job_rf[:], first, AX.X, ALU.add))
            link(dve.tensor_reduce(job_xf[:], past_end, AX.X, ALU.add))
            link(dve.tensor_scalar_min(job_xf[:], job_xf[:], float(X - 1)))
            link(dve.tensor_scalar_mul(job_sf[:], past_end[:, :, X - 1], float(SPARE)))
            link(dve.tensor_tensor(job_rf[:], job_rf[:], job_sf[:], ALU.add))
            dve.tensor_copy(job_x[:], job_xf[:]).then_inc(s_pl, 1)
            dve.tensor_copy(job_row[:], job_rf[:]).then_inc(s_pl, 1)

    experts(nc, B, T, E, X, F, ROW, SPARE, JOBS, xs_dram, y_dram, x1_dram, out,
            job_x, job_row, w13, w2s, ident, eps_col)
    keep.close()


def experts(nc, B, T, E, X, F, ROW, SPARE, JOBS, xs_dram, y_dram, x1_dram, out,
            job_x, job_row, w13, w2s, ident, eps_col):
    TT = T // P
    TOP = 2
    FC = F // P
    TOKENS = B * T
    XR = 8
    YR = 8
    TR = 4
    AHEAD = 2
    ctx = ExitStack()
    with ctx:
        def sb(name, shape, dt=FP32):
            return ctx.enter_context(nc.sbuf_tensor(name, shape, dt))

        def ps(name, shape, dt=FP32):
            return ctx.enter_context(nc.psum_tensor(name, shape, dt))

        def sem(name):
            return ctx.enter_context(nc.semaphore(name))

        def sems(name, n):
            return [sem(f"{name}{i}") for i in range(n)]

        rows = sb("rows", [P, XR, ROW])
        rowsT = sb("rowsT", [E, TR, P])
        gate = sb("gate", [P, 2, F])
        hid = sb("hid", [P, 2, F])
        hidT = sb("hidT", [P, 2, FC, P])
        res = sb("res", [P, YR, E])
        res_to = sb("res_to", [P, YR], UINT32)
        RB = 4
        NB = 8
        xa = sb("xa", [P, B, TT, E])
        ya = sb("ya", [P, NB, TOP, TT, E])
        yy = sb("yy", [P, RB, TT, E])
        tot = sb("tot", [P, RB, TT, E])
        stats = sb("stats2", [P, TT, 6])
        mean_var = sb("mean_var2", [P, RB, TT, 2])
        log_var = sb("log_var2", [P, RB, TT])
        rstd = sb("rstd2", [P, RB, TT])
        shift = sb("shift", [P, RB, TT])
        fin = sb("fin", [P, RB, TT, E])

        psX = ps("psX", [P, 2, T])
        psH = ps("psH", [P, 2, T])
        psT = ps("psT", [P, 2, T])
        psY = ps("psY", [P, 2, T])

        s_passed_pool = sem("pool_passed2")
        s_x = sems("rows_loaded", XR)
        s_xt = sem("rows_transposed")
        s_xc = sem("rowsT_copied")
        s_h = sem("hidden_ready")
        s_g = sem("gate_made")
        s_m = sem("hidden_made")
        s_ht = sem("hidden_transposed")
        s_hc = sem("hiddenT_copied")
        s_y = sem("result_ready")
        s_to = sem("destination_made")
        s_yc = sem("result_scaled")
        s_sc = sems("result_scattered", YR)
        s_l = sems("results_loaded", NB)
        s_xa = sem("x1_loaded")
        s_a1 = sem("results_added")
        s_a2 = sem("total_made")
        s_st = sem("stats_made2")
        s_mv = sem("mean_var_made2")
        s_lg = sem("log_made2")
        s_rs = sem("rstd_made2")
        s_sh = sem("shift_made")
        s_f = sem("final_made")
        s_o = sems("out_stored", RB)

        x_v = x1_dram.rearrange("(b i p) e -> b p i e", p=P, i=TT)
        y_v = y_dram.rearrange("(j b i p) e -> j b p i e", p=P, i=TT, j=TOP)
        o_v = out.rearrange("b (i p) e -> b p i e", p=P)

        def over_jobs(eng, step, lead, lag):
            lo, hi = 2 * XR, JOBS - XR
            for n in range(-lead, lo):
                step(n, n % XR)
            with eng.Fori(0, (hi - lo) // XR) as i:
                for u in range(XR):
                    step(i * XR + lo + u, u)
            for n in range(lo + (hi - lo) // XR * XR, JOBS + lag):
                step(n, n % XR)

        def is_job(n):
            return not isinstance(n, int) or 0 <= n < JOBS

        block = ctx.enter_context(nc.Block())

        @block.sync
        def _(sp):
            def step(n, u):
                if is_job(n):
                    wait(sp, s_yc, n - XR + 1)
                    row = sp.value_load(job_row[0:1, bass.ds(n, 1)], min_val=0, max_val=SPARE)
                    sp.dma_start(rows[:, u, :], xs_dram[bass.ds(row, P), :]).then_inc(s_x[u], 16)
                if isinstance(n, int) and n < 2 * XR:
                    for b in range(n, B, 2 * XR):
                        sp.dma_start(xa[:, b], x_v[b]).then_inc(s_xa, 16)

            over_jobs(sp, step, 0, 0)
            for u in range(YR):
                sp.wait_ge(s_sc[u], 16 * len(range(u, JOBS, YR)))
            for b in range(B):
                wait(sp, s_a1, b - NB + 1)
                for j in range(TOP):
                    sp.dma_start(ya[:, b % NB, j], y_v[j, b]).then_inc(s_l[b % NB], 16)
            for b in range(B):
                sp.wait_ge(s_f, b + 1)
                sp.dma_start(o_v[b], fin[:, b % RB]).then_inc(s_o[b % RB], 16)
            for u in range(RB):
                sp.wait_ge(s_o[u], 16 * len(range(u, B, RB)))

        @block.gpsimd
        def _(pool):
            def step(n, u):
                if is_job(n):
                    wait_apart(pool, s_yc, n + 1, s_passed_pool)
                    wait_apart(pool, s_to, n + 1, s_passed_pool)
                    pool.indirect_dma_start(out=y_dram, out_offset=bass.IndirectOffsetOnAxis(ap=res_to[:, u:u + 1], axis=0),
                                            in_=res[:, u, :], in_offset=None, bounds_check=TOP * TOKENS - 1,
                                            oob_is_err=False).then_inc(s_sc[u], 16)
            over_jobs(pool, step, 0, 0)

            for b in range(B):
                pool.wait_ge(s_l[b % NB], TOP * 16 * (b // NB + 1))
                wait(pool, s_a2, b - RB + 1)
                pool.tensor_tensor(yy[:, b % RB], ya[:, b % NB, 0], ya[:, b % NB, 1], ALU.add).then_inc(s_a1, 1)

        @block.tensor
        def _(pe):
            loaded = {}

            def expert_of(n, u, k):
                if not isinstance(n, int) and u == 0 and k == 0:
                    loaded.clear()
                key = n + k if isinstance(n, int) else ("turn", u + k)
                if key not in loaded:
                    loaded[key] = pe.value_load(job_x[0:1, bass.ds(n + k, 1)], min_val=0, max_val=X - 1)
                return loaded[key]

            def step(n, u):
                v = u % 2
                ahead, back, back2 = n + AHEAD, n - 1, n - 2
                if is_job(ahead):
                    a = (u + AHEAD) % XR
                    pe.wait_ge(s_x[a], rounds(ahead, a))
                    wait(pe, s_xc, ahead - 1)
                    pe.transpose(psX[:, a % 2, 0:P], rows[:, a, 0:E], ident[:]).then_inc(s_xt, 1)
                if is_job(n):
                    x = expert_of(n, u, 0)
                    pe.wait_ge(s_xc, n + 1)
                    wait(pe, s_m, n - 1)
                    pe.matmul(psH[:, v, :], rowsT[:, u % TR, :], w13[:, bass.ds(x, 1), :].rearrange("p o f -> p (o f)"),
                              start=True, stop=True).then_inc(s_h, 1)
                if is_job(back2):
                    x2 = expert_of(n, u, -2)
                if is_job(n + 1) and (isinstance(n, int) or u + 1 < XR):
                    expert_of(n, u, 1)
                if is_job(back):
                    pe.wait_ge(s_m, back + 1)
                    wait(pe, s_hc, back - 1)
                    for c in range(FC):
                        last = pe.transpose(psT[:, 1 - v, P * c:P * c + P], hid[:, 1 - v, P * c:P * c + P], ident[:])
                    last.then_inc(s_ht, 1)
                if is_job(back2):
                    pe.wait_ge(s_hc, back2 + 1)
                    wait(pe, s_yc, back2 - 1)
                    for c in range(FC):
                        last = pe.matmul(psY[:, v, 0:E], hidT[:, v, c, :], w2s[:, bass.ds(x2, 1), c, :].rearrange("p o e -> p (o e)"),
                                         start=c == 0, stop=c == FC - 1)
                    last.then_inc(s_y, 1)

            def rounds(n, u):
                if isinstance(n, int):
                    return 16 * (n // XR + 1)
                return (n - (u % XR)) * (16 // XR) + 16
            over_jobs(pe, step, AHEAD, 2)

        @block.scalar
        def _(act):
            act.preload_act_table(ACT.Silu)

            def step(n, u):
                v = u % 2
                ahead, back2 = n + AHEAD, n - 2
                if is_job(ahead):
                    a = (u + AHEAD) % XR
                    act.wait_ge(s_xt, ahead + 1)
                    wait(act, s_h, ahead - TR + 1)
                    act.activation(rowsT[:, a % TR, :], psX[:, a % 2, 0:P], ACT.Copy).then_inc(s_xc, 1)
                if is_job(n):
                    act.wait_ge(s_h, n + 1)
                    wait(act, s_m, n - 1)
                    act.activation(gate[:, v, :], psH[:, v, 0:F], ACT.Silu).then_inc(s_g, 1)
                if is_job(back2):
                    w = (u - 2) % YR
                    act.wait_ge(s_y, back2 + 1)
                    if not isinstance(back2, int) or back2 >= YR:
                        act.wait_ge(s_sc[w], rounds(back2, w) - 16)
                    act.activation(res[:, w, :], psY[:, v, 0:E], ACT.Copy, scale=rows[:, w, E:E + 1]).then_inc(s_yc, 1)

            def rounds(n, u):
                if isinstance(n, int):
                    return 16 * (n // YR + 1)
                return (n - (u % YR)) * (16 // YR) + 16
            over_jobs(act, step, AHEAD, 2)
            act.preload_act_table_set("natural_log_exp_and_others")
            def scale(b):
                act.wait_ge(s_mv, b + 1)
                act.activation(log_var[:, b % RB], mean_var[:, b % RB, :, 1], ACT.Ln, bias=eps_col[:]).then_inc(s_lg, 1)
                act.wait_ge(s_lg, b + 1)
                act.activation(rstd[:, b % RB], log_var[:, b % RB], ACT.Exp, scale=-0.5).then_inc(s_rs, 1)

            def normalize(b):
                act.wait_ge(s_sh, b + 1)
                if b >= RB:
                    act.wait_ge(s_o[b % RB], 16 * (b // RB))
                for i in range(TT):
                    last = act.activation(fin[:, b % RB, i], tot[:, b % RB, i], ACT.Identity, bias=shift[:, b % RB, i:i + 1],
                                          scale=rstd[:, b % RB, i:i + 1])
                last.then_inc(s_f, 1)

            for b in range(B):
                scale(b)
                if b:
                    normalize(b - 1)
            normalize(B - 1)
        @block.vector
        def _(dve):
            def step(n, u):
                v = u % 2
                back = n - 1
                if is_job(n):
                    w = u % YR
                    if not isinstance(n, int) or n >= YR:
                        dve.wait_ge(s_sc[w], rounds(n, w) - 16)
                    dve.wait_ge(s_h, n + 1)
                    dve.tensor_copy(res_to[:, w:w + 1], rows[:, u, E + 1:E + 2]).then_inc(s_to, 1)
                    dve.wait_ge(s_g, n + 1)
                    wait(dve, s_ht, n - 1)
                    dve.tensor_tensor(hid[:, v, :], gate[:, v, :], psH[:, v, F:2 * F], ALU.mult).then_inc(s_m, 1)
                if is_job(back):
                    dve.wait_ge(s_ht, back + 1)
                    wait(dve, s_y, back - 1)
                    dve.tensor_copy(hidT[:, 1 - v].rearrange("p c t -> p (c t)"), psT[:, 1 - v, 0:F]).then_inc(s_hc, 1)

            def rounds(n, u):
                if isinstance(n, int):
                    return 16 * (n // YR + 1)
                return (n - (u % YR)) * (16 // YR) + 16
            over_jobs(dve, step, 0, 1)

            def total(b):
                dve.wait_ge(s_a1, b + 1)
                wait(dve, s_f, b - RB + 1)
                dve.tensor_tensor(tot[:, b % RB], xa[:, b], yy[:, b % RB], ALU.add).then_inc(s_a2, 1)
                dve.wait_ge(s_a2, b + 1)
                for i in range(TT):
                    last = dve.bn_stats(stats[:, i], tot[:, b % RB, i])
                last.then_inc(s_st, 1)
                dve.wait_ge(s_st, b + 1)
                for i in range(TT):
                    last = dve.bn_aggr(mean_var[:, b % RB, i], stats[:, i])
                last.then_inc(s_mv, 1)

            def shift_of(b):
                dve.wait_ge(s_rs, b + 1)
                dve.scalar_tensor_tensor(out=shift[:, b % RB], in0=mean_var[:, b % RB, :, 0], scalar=-1.0, in1=rstd[:, b % RB],
                                         op0=ALU.mult, op1=ALU.mult).then_inc(s_sh, 1)

            dve.wait_ge(s_xa, 16 * B)
            for b in range(B):
                total(b)
                if b:
                    shift_of(b - 1)
            shift_of(B - 1)


_INS = ["L0_attn_hidden_states", "L0_attn_Wq", "L0_attn_Wk_down", "L0_attn_Wv_down", "L0_attn_q_to_latent",
        "L0_attn_v_up", "L0_attn_Wout", "L0_ffn_w_gate", "L0_ffn_w1", "L0_ffn_w3", "L0_ffn_w2"]


def kernel(**inputs):
    import numpy as _np
    import concourse.bacc as _bacc
    from concourse.bass_utils import run_bass_kernel_spmd as _run

    nc = _bacc.Bacc("TRN2", target_bir_lowering=False, num_devices=1)
    arrays, args = {}, []
    for name in _INS:
        a = _np.ascontiguousarray(inputs[name])
        arrays[f"in_{name}_dram"] = a
        args.append(nc.dram_tensor(f"in_{name}_dram", a.shape, mybir.dt.from_np(a.dtype), kind="ExternalInput").ap())
    shape = inputs[_INS[0]].shape
    out = nc.dram_tensor("out_dram", shape, FP32, kind="ExternalOutput").ap()
    build(nc, *args, out)
    r = _run(nc, [arrays], core_ids=[0])
    return r.results[0]["out_dram"]
```

```python
import concourse.bass as bass
from concourse import mybir
from contextlib import ExitStack

FP32 = mybir.dt.float32
BF16 = mybir.dt.bfloat16
INT32 = mybir.dt.int32
UINT32 = mybir.dt.uint32
ALU = mybir.AluOpType
ACT = mybir.ActivationFunctionType
AX = mybir.AxisListType

P = 128
NEG = -1e30
EPS = 1e-5
PARTS = 3
Q_ROWS = [(0, 0, 3), (3, 1, 2), (5, 2, 1)]
K_ROWS = [(0, 0, 3), (3, 0, 2), (5, 0, 1)]
MAX_ROW = 96
STACK = 3


class Batch:

    def __init__(self, turns, off, count):
        self.turns, self.off, self.count = turns, off, count
        self.num = turns * STACK + off
        self.buf = off % STACK
        self.round = turns + off // STACK

    def plus(self, k):
        return Batch(self.turns, self.off + k, self.count)

    @property
    def exists(self):
        return not isinstance(self.num, int) or 0 <= self.num < self.count


def wait(eng, sem, value):
    if not isinstance(value, int) or value > 0:
        eng.wait_ge(sem, value)


def wait_apart(eng, sem, value, passed):
    if not isinstance(value, int):
        eng.wait_ge(sem, value)
        eng.sem_inc(passed, 1)
    elif value > 0:
        eng.wait_ge(sem, value)


def over_batches(eng, count, step):
    full_from, full_to = 3, count - 3
    turns = (full_to - full_from) // STACK
    for b in range(-2, full_from):
        step(Batch(0, b, count))
    if turns:
        with eng.Fori(0, turns) as i:
            for u in range(STACK):
                step(Batch(i, full_from + u, count))
    for b in range(full_from + turns * STACK, count + 2):
        step(Batch(0, b, count))


def build(nc, hidden, Wq, Wk_down, Wv_down, q_to_latent, v_up, Wout, w_gate, w1, w3, w2, out):
    B, T, E = hidden.shape
    H, D, L = q_to_latent.shape
    TT = T // P
    QUAD = 4
    QUADS = H // QUAD
    HP = QUAD // 2
    EB = 10
    MB = EB // 2
    CT = 32
    SC = float(L) ** -0.5
    X = w_gate.shape[1]
    TOP = 2
    F = w1.shape[2]
    FC = F // P
    TOKENS = B * T
    REGION = TOKENS + P
    ROW = E + 2
    SPARE = X * REGION
    JOBS = -(-(TOP * TOKENS + X * (P - 1)) // P)
    JOBS += JOBS % 2
    NOWHERE = float(4 * TOKENS)

    xs_dram = nc.dram_tensor("expert_rows", (SPARE + P, ROW), FP32, kind="Internal").ap()
    y_dram = nc.dram_tensor("expert_results", (TOP * TOKENS, E), FP32, kind="Internal").ap()
    x1_dram = nc.dram_tensor("x1", (TOKENS, E), FP32, kind="Internal").ap()

    keep = ExitStack()
    base = keep.enter_context(nc.sbuf_tensor("next_row", [P, X], FP32))
    ident = keep.enter_context(nc.sbuf_tensor("ident", [P, P], FP32))
    eps_col = keep.enter_context(nc.sbuf_tensor("eps_col", [P, 1], FP32))
    region0 = keep.enter_context(nc.sbuf_tensor("region0", [P, X], FP32))
    job_x = keep.enter_context(nc.sbuf_tensor("job_x", [1, JOBS], INT32))
    job_row = keep.enter_context(nc.sbuf_tensor("job_row", [1, JOBS], INT32))
    probs = keep.enter_context(nc.sbuf_tensor("probs", [P, 2, EB, T], FP32))
    w13 = probs[:, 0].rearrange("p k t -> p (k t)")[:, 0:X * 2 * F].rearrange("p (x f) -> p x f", x=X)
    w2s = probs[:, 1].rearrange("p k t -> p (k t)")[:, 0:F * X * E // P].rearrange("p (x c e) -> p x c e", x=X, e=E)

    ctx = ExitStack()
    with ctx:
        def sb(name, shape, dt=FP32):
            return ctx.enter_context(nc.sbuf_tensor(name, shape, dt))

        def ps(name, shape, dt=FP32):
            return ctx.enter_context(nc.psum_tensor(name, shape, dt))

        def sem(name):
            return ctx.enter_context(nc.semaphore(name))

        def sems(name, n):
            return [sem(f"{name}{i}") for i in range(n)]

        def dram(name, shape, dt=FP32):
            return nc.dram_tensor(name, shape, dt, kind="Internal").ap()

        parts_dram = [[dram(f"parts_{w}{i}", (PARTS, D, H, T), BF16) for i in range(STACK)] for w in "qk"]
        heads_dram = [dram(f"heads_{i}", (H, D + 1, T)) for i in range(STACK)]
        recip_dram = [dram(f"recip_{i}", (H, T)) for i in range(STACK)]

        ident_bf = sb("ident_bf", [P, P], BF16)
        ahead = sb("ahead", [P, 2, P], BF16)
        wq_nat = sb("wq_nat", [P, E])
        wout_nat = sb("wout_nat", [P, E])
        qtl_nat = sb("qtl_nat", [P, L])
        wkd = sb("wkd", [L, E])
        wvd = sb("wvd", [L, E])
        vup = sb("vup", [L, H, D])
        qtlT = sb("qtlT", [L, P])
        wqT = sb("wqT", [P, H * D])
        wkT = sb("wkT", [P, H * D])
        wvT = sb("wvT", [P, H * D])
        woutT = sb("woutT", [P, E])
        x_in = sb("x_in", [P, STACK, TT, E])
        x_res = sb("x_res", [P, STACK, TT, E])
        xT = sb("xT", [P, T])
        qk_parts = [sb("q_parts", [P, PARTS, T], BF16), sb("k_parts", [P, PARTS, T], BF16)]
        qk_rest = [sb("q_rest", [P, T]), sb("k_rest", [P, T])]
        q_stack = [sb(f"q_stack{i}", [P, H, T], BF16) for i in range(STACK)]
        k_stack = [sb(f"k_stack{i}", [P, H, T], BF16) for i in range(STACK)]
        v_aug = sb("v_aug", [P, STACK, TT * H * 2 * D + CT - 2 * D])
        part_max = sb("part_max", [P, QUADS * HP, 5, 4])
        row_max = sb("row_max", [P, H, TT])
        max_parts = sb("max_parts", [H * TT, PARTS, P], BF16)
        max_rest = sb("max_rest", [H * TT, P])
        heads_out = sb("heads_out", [P, QUADS, T])
        numer = sb("numer", [P, T])
        denom = sb("denom", [P, T * H // P])
        rden = sb("rden", [P, T * H // P])
        rden_all = sb("rden_all", [P, T])
        headsT = sb("headsT", [P, T])
        stats = sb("stats", [P, TT, 6])
        mean_var = sb("mean_var", [P, TT, 2])
        log_var = sb("log_var", [P, TT])
        rstd = sb("rstd", [P, TT])
        image = sb("image", [P, TT, TOP, ROW])
        x1T = xT
        wg = sb("wg", [E, X])
        before = sb("before", [P, P], BF16)
        ones_bf = sb("ones_bf", [P, P], BF16)
        before_f = sb("before_f", [P, P])
        iota_i = sb("iota_i", [P, X], INT32)
        iota_x = sb("iota_x", [P, X])
        dest_i = sb("dest_i", [P, TT * TOP], INT32)
        dest = sb("dest", [P, TT, TOP])
        logits = sb("logits", [P, TT, X])
        top = sb("top", [P, TT, 8])
        top_at = sb("top_at", [P, TT, 8], UINT32)
        top_f = sb("top_f", [P, TT, TOP])
        chosen_bf = sb("chosen_bf", [P, TT, TOP, X], BF16)
        gap = sb("gap", [P, TT])
        odds = sb("odds", [P, TT])
        odds1 = sb("odds1", [P, TT])
        row_of = sb("row_of", [P, TT, X])
        picked = sb("picked", [P, TT, TOP, X])
        row_f = sb("row_f", [P, TT, TOP])
        row_i = sb("row_i", [P, TT, TOP], UINT32)
        iota_ji = sb("iota_ji", [1, JOBS], INT32)
        iota_j = sb("iota_j", [1, JOBS])
        rows_n = sb("rows_n", [P, X])
        tiles_i = sb("tiles_i", [P, X], INT32)
        tiles = sb("tiles", [P, X])
        ones_x = sb("ones_x", [P, X])
        tile_end = sb("tile_end", [P, X])
        tile_start = sb("tile_start", [P, X])
        lead = sb("lead", [P, X + 1])
        lead_step = sb("lead_step", [P, X])
        job_xf = sb("job_xf", [1, JOBS])
        job_rf = sb("job_rf", [1, JOBS])
        job_sf = sb("job_sf", [1, JOBS])
        pad_i = sb("pad_i", [P, X], INT32)
        padding = sb("padding", [P, ROW])
        values_flat = v_aug[0:1].rearrange("p s n -> p (s n)")
        past_end, steps_past = [values_flat[:, n * JOBS * X:(n + 1) * JOBS * X].rearrange("p (j x) -> p j x", x=X)
                                for n in range(2)]

        score = ps("score", [P, 2, T])
        maxs = ps("maxs", [P, 2, 2, T])
        attn = ps("attn", [P, T])
        misc = ps("misc", [P, T])

        s_passed_pool, s_passed_dve, s_passed_pe = sem("pool_passed"), sem("dve_passed"), sem("pe_passed")
        s_w = sem("weights_loaded")
        s_const = sem("constants_made")
        s_wt = sem("weight_product_done")
        s_wc = sem("weight_copied")
        s_zero = sems("stacks_cleared", STACK)
        s_vones = sem("v_ones_made")
        s_xin = sems("x_in_loaded", STACK)
        s_xres = sems("x_res_loaded", STACK)
        s_xt = sem("x_transposed")
        s_xtc = sem("xT_copied")
        s_proj = sem("q_or_k_projected")
        s_hi = sem("part0_made")
        s_mid = sem("part1_made")
        s_rest = sem("rest_made")
        s_parts = sem("parts_made")
        s_pst = [sems("q_parts_stored", STACK), sems("k_parts_stored", STACK)]
        s_stk = sems("stack_loaded", STACK)
        s_v = sem("v_projected")
        s_vc = sem("v_copied")
        s_msc = sem("scores_for_max_ready")
        s_mx = sem("block_maxima_taken")
        s_rm = sem("row_max_combined")
        s_nmt = sem("row_max_transposed")
        s_nm0 = sem("max_part0_made")
        s_nmr = sem("max_rest_made")
        s_nm1 = sem("max_part1_made")
        s_nmp = sem("max_parts_made")
        s_nmd = sems("max_rows_loaded", STACK)
        s_sc = sem("scores_ready")
        s_exp = sem("exp_done")
        s_tri = sem("future_cleared")
        s_pv = sem("quad_attended")
        s_oc = sem("quad_copied")
        s_hd = sems("heads_stored", STACK)
        s_nd = sems("numer_denom_loaded", STACK)
        s_rd = sem("recip_made")
        s_rst = sems("recip_stored", STACK)
        s_rl = sems("recip_loaded", STACK)
        s_ht = sem("heads_normalized")
        s_op = sem("out_projected")
        s_res = sem("residual_added")
        s_st = sem("stats_step")
        s_ln = sem("log_made")
        s_rs = sem("rstd_made")
        s_x1 = sem("x1_made")
        s_out = sem("x1_stored")
        s_x1t = sem("x1_transposed")
        s_x1tc = sem("x1T_copied")
        s_lg = sem("logits_ready")
        s_ch = sem("choice_step")
        s_oh = sem("choice_made")
        s_gap = sem("gap_made")
        s_odds = sem("odds_made")
        s_rk = sem("ranks_ready")
        s_rr = sem("ranks_read")
        s_ro = sem("row_step")
        s_im = sem("image_doubled")
        s_rows = sem("rows_made")
        s_sct = sem("rows_scattered")
        s_pl = sem("plan_step")
        s_plan0 = sem("plan_constants_made")
        s_past = sem("jobs_past_end_step")
        s_padi = sem("padding_rows_known")
        s_pad = sem("padding_stored")
        s_ew = sem("expert_weights_loaded")

        WEIGHTS = 8 * 16
        def exps(b, g, k):
            return (b.num * QUADS + g) * EB + k + 1
        def maxes(b, g, k):
            return (b.num * QUADS + g) * MB + k + 1
        TRI = 6
        def quad(b, g):
            return b.num * QUADS + g

        x_dram = hidden.rearrange("b (i p) e -> b p i e", p=P)
        x1_v = x1_dram.rearrange("(b i p) e -> b p i e", p=P, i=TT)


        BF16_ONES = 1.0 + 0x3F80 / 2 ** 23

        def clear_stacks(eng, i):
            for stack in (q_stack[i], k_stack[i]):
                eng.memset(stack[0:MAX_ROW].rearrange("p h t -> p (h t)").bitcast(FP32), 0.0).then_inc(s_zero[i], 1)
            eng.wait_ge(s_zero[i], 2)
            eng.memset(k_stack[i][MAX_ROW:P].rearrange("p h t -> p (h t)").bitcast(FP32), BF16_ONES).then_inc(s_zero[i], 1)
            eng.wait_ge(s_zero[i], 3)

        block = ctx.enter_context(nc.Block())

        @block.sync
        def _(sp):
            sp.dma_start(x_in[:, 0], x_dram[0]).then_inc(s_xin[0], 16)
            sp.dma_start(wq_nat[:], Wq).then_inc(s_w, 16)
            sp.dma_start(wout_nat[:], Wout).then_inc(s_w, 16)
            sp.dma_start(qtl_nat[:], q_to_latent.rearrange("h d l -> (h d) l")).then_inc(s_w, 16)
            sp.dma_start(wkd[:], Wk_down).then_inc(s_w, 16)
            sp.dma_start(wg[:], w_gate).then_inc(s_w, 16)
            sp.dma_start(wvd[:], Wv_down).then_inc(s_w, 16)
            sp.dma_start(vup[:, 0:H // 2], v_up[0:H // 2].rearrange("h l d -> l h d")).then_inc(s_w, 16)
            sp.dma_start(vup[:, H // 2:H], v_up[H // 2:H].rearrange("h l d -> l h d")).then_inc(s_w, 16)

            def store_parts(b, w):
                sp.wait_ge(s_parts, 2 * b.num + w + 1)
                for p in range(PARTS):
                    sp.dma_start(parts_dram[w][b.buf][p].rearrange("d h t -> h d t"), qk_parts[w][:, p, :])\
                      .then_inc(s_pst[w][b.buf], 16)

            def load_stack(b, w):
                parts, rows, stack = parts_dram[w][b.buf], (Q_ROWS, K_ROWS)[w], (q_stack, k_stack)[w][b.buf]
                sp.wait_ge(s_pst[w][b.buf], PARTS * 16 * (b.round + 1))
                sp.wait_ge(s_zero[b.buf], 3)
                wait(sp, s_sc, exps(b.plus(-STACK), QUADS - 1, EB - 1))
                for first, part, n in rows:
                    dst = stack[first * D:(first + n) * D].rearrange("p h t -> p (h t)")
                    if w == 0:
                        src = parts[part:part + 1].rearrange("o d h t -> o d (h t)").broadcast_to([n, D, H * T])
                    else:
                        src = parts[part:part + n].rearrange("o d h t -> (o d) (h t)")
                    sp.dma_start(dst, src).then_inc(s_stk[b.buf], 16)

            def step(b):
                done, prev, nxt, far = b.plus(-2), b.plus(-1), b.plus(1), b.plus(2)
                coming = b.plus(3)
                if coming.exists:
                    wait(sp, s_xt, coming.num - STACK + 1)
                    sp.dma_start(x_in[:, coming.buf], x_dram[coming.num]).then_inc(s_xin[coming.buf], 16)
                if prev.exists:
                    sp.dma_start(x_res[:, prev.buf], x_dram[prev.num]).then_inc(s_xres[prev.buf], 16)
                if done.exists:
                    sp.wait_ge(s_x1, done.num + 1)
                    sp.dma_start(x1_v[done.num], image[:, :, 0, 0:E]).then_inc(s_out, 16)
                if far.exists:
                    store_parts(far, 0)
                    if not prev.exists:
                        store_parts(far, 1)
                if prev.exists:
                    sp.wait_ge(s_oc, quad(prev, QUADS - 1) + 1)
                    dst = heads_dram[prev.buf].rearrange("(g q) r t -> q r g t", q=QUAD)
                    for q in range(QUAD):
                        sp.dma_start(dst[q], heads_out[CT * q:CT * q + D + 1]).then_inc(s_hd[prev.buf], 16)
                if far.exists:
                    load_stack(far, 0)
                if prev.exists:
                    sp.wait_ge(s_hd[prev.buf], QUAD * 16 * (prev.round + 1))
                    wait(sp, s_ht, prev.num)
                    sp.dma_start(denom[:], heads_dram[prev.buf][:, D, :].rearrange("h (c t) -> h c t", c=D))\
                      .then_inc(s_nd[prev.buf], 16)
                    sp.dma_start(numer[:], heads_dram[prev.buf][:, 0:D, :]).then_inc(s_nd[prev.buf], 16)
                if far.exists:
                    if prev.exists:
                        store_parts(far, 1)
                    load_stack(far, 1)
                if prev.exists:
                    sp.wait_ge(s_rd, prev.num + 1)
                    sp.dma_start(recip_dram[prev.buf].rearrange("h (c t) -> h c t", c=D), rden[:])\
                      .then_inc(s_rst[prev.buf], 16)
                    sp.wait_ge(s_rst[prev.buf], 16 * (prev.round + 1))
                    sp.dma_start(rden_all[:],
                                 recip_dram[prev.buf].rearrange("h (o t) -> h o t", o=1).broadcast_to([H, D, T]))\
                      .then_inc(s_rl[prev.buf], 16)
                if nxt.exists:
                    for p in range(PARTS):
                        sp.wait_ge((s_nm0, s_nm1, s_nmp)[p], nxt.num + 1)
                        sp.dma_start(q_stack[nxt.buf][MAX_ROW + p:MAX_ROW + p + 1].rearrange("o h (i t) -> o (h i) t", i=TT),
                                     max_parts[:, p, :]).then_inc(s_nmd[nxt.buf], 16)

            over_batches(sp, B, step)
            sp.wait_ge(s_pv, QUADS * B)
            sp.dma_start(w13[:, :, 0:F], w1.rearrange("x e f -> e x f")).then_inc(s_ew, 16)
            sp.dma_start(w13[:, :, F:2 * F], w3.rearrange("x e f -> e x f")).then_inc(s_ew, 16)
            sp.dma_start(w2s.rearrange("p x c e -> p (x c) e"), w2.rearrange("x (c p) e -> p (x c) e", p=P)).then_inc(s_ew, 16)
            sp.wait_ge(s_const, 16)
            sp.dma_start(xs_dram[SPARE:SPARE + P, :], padding[:]).then_inc(s_pad, 16)
            sp.wait_ge(s_padi, 1)
            for x in range(X):
                row = sp.value_load(pad_i[0:1, x:x + 1], min_val=0, max_val=SPARE - P)
                sp.dma_start(xs_dram[bass.ds(row, P), :], padding[:]).then_inc(s_pad, 16)
            sp.wait_ge(s_pad, 16 * (X + 1))
            sp.wait_ge(s_ew, 48)
            sp.wait_ge(s_out, 16 * B)

        @block.gpsimd
        def _(pool):
            pool.memset(ident[:], 0.0).then_inc(s_const, 1)
            pool.memset(ahead[:], 0.0).then_inc(s_const, 1)
            pool.wait_ge(s_const, 2)
            pool.affine_select(out=ident[:], in_=ident[:], compare_op=ALU.not_equal, fill=1.0, base=0,
                               pattern=[[-1, P]], channel_multiplier=1).then_inc(s_const, 1)
            pool.affine_select(out=ahead[:], in_=ahead[:], compare_op=ALU.is_ge, fill=NEG, base=0,
                               pattern=[[0, 2], [-1, P]], channel_multiplier=1).then_inc(s_const, 1)
            pool.wait_ge(s_const, 4)
            pool.tensor_copy(ident_bf[:], ident[:]).then_inc(s_const, 1)
            pool.memset(eps_col[:], EPS).then_inc(s_const, 1)
            pool.memset(ones_bf[:], 1.0).then_inc(s_const, 1)
            pool.memset(before_f[:], 1.0).then_inc(s_const, 1)
            pool.iota(iota_i[:], pattern=[[1, X]], base=0, channel_multiplier=0).then_inc(s_const, 1)
            pool.iota(dest_i[:], pattern=[[P, TT], [TOKENS, TOP]], base=0, channel_multiplier=1).then_inc(s_const, 1)
            pool.wait_ge(s_const, 10)
            pool.affine_select(out=before_f[:], in_=before_f[:], compare_op=ALU.is_gt, fill=0.0, base=0,
                               pattern=[[1, P]], channel_multiplier=-1).then_inc(s_const, 1)
            pool.wait_ge(s_const, 11)
            pool.tensor_copy(before[:], before_f[:]).then_inc(s_const, 1)
            pool.iota(iota_ji[:], pattern=[[1, JOBS]], base=0, channel_multiplier=0).then_inc(s_const, 1)
            pool.memset(ones_x[:], 1.0).then_inc(s_const, 1)
            pool.memset(padding[:], 0.0).then_inc(s_const, 1)
            pool.wait_ge(s_const, 15)
            pool.memset(padding[:, E + 1:E + 2], NOWHERE).then_inc(s_const, 1)
            clear_stacks(pool, 0)

            def step(b):
                prev, far, done = b.plus(-1), b.plus(2), b.plus(-2)
                if isinstance(b.num, int) and 0 < far.num < STACK:
                    clear_stacks(pool, far.num)

                def clear_future(g, pr):
                    pt = probs[:, g % 2]
                    both = pt[:, 5 * pr + 4, :].rearrange("p (e t) -> p e t", e=2)[:, :, 0:P]
                    odd = pt[:, 5 * pr + 2:5 * pr + 4, 0:2 * P].rearrange("p e (i t) -> p e i t", i=2)
                    for n, (last_unit, blocks, pattern) in enumerate((
                            (1, pt[:, 5 * pr:5 * pr + 2, 0:P], [[0, 2], [1, P]]),
                            (3, odd, [[0, 2], [0, 2], [1, P]]),
                            (4, both, [[0, 2], [1, P]]))):
                        if b.exists:
                            wait_apart(pool, s_exp, exps(b, g, 5 * pr + last_unit), s_passed_pool)
                            pool.affine_select(out=blocks, in_=blocks, compare_op=ALU.is_ge, fill=0.0, base=0,
                                               pattern=pattern, channel_multiplier=-1).then_inc(s_tri, 1)
                        place = 3 * (HP * g + pr) + n - (3 * HP * QUADS - TT * TOP)
                        if place >= 0 and done.exists:
                            scatter(place)

                def last_part(w):
                    wait_apart(pool, s_mid, 2 * far.num + w + 1, s_passed_pool)
                    pool.tensor_tensor(qk_parts[w][:, 2, :], qk_rest[w][:], qk_parts[w][:, 1, :], ALU.subtract)\
                        .then_inc(s_parts, 1)

                def scatter(n):
                    if n == 0:
                        wait_apart(pool, s_rows, done.num + 1, s_passed_pool)
                        wait_apart(pool, s_im, done.num + 1, s_passed_pool)
                    i, j = n // TOP, n % TOP
                    pool.indirect_dma_start(
                        out=xs_dram, out_offset=bass.IndirectOffsetOnAxis(ap=row_i[:, i, j:j + 1], axis=0),
                        in_=image[:, i, j, :], in_offset=None).then_inc(s_sct, 16)

                for g in range(QUADS):
                    for pr in range(HP):
                        clear_future(g, pr)
                        if (g, pr) in ((0, 1), (1, 0)) and far.exists:
                            last_part(g)
                        if (g, pr) == (1, 1) and done.exists:
                            wait_apart(pool, s_x1, done.num + 1, s_passed_pool)
                            pool.tensor_copy(image[:, :, 1, 0:E], image[:, :, 0, 0:E]).then_inc(s_im, 1)
                        if (g, pr) == ((2, 1) if b.exists else (3, 0)) and prev.exists:
                            wait_apart(pool, s_rl[prev.buf], 16 * (prev.round + 1), s_passed_pool)
                            wait_apart(pool, s_nd[prev.buf], 2 * 16 * (prev.round + 1), s_passed_pool)
                            wait_apart(pool, s_op, prev.num, s_passed_pool)
                            pool.tensor_tensor(headsT[:], numer[:], rden_all[:], ALU.mult).then_inc(s_ht, 1)

            over_batches(pool, B, step)
            pool.wait_ge(s_sct, TT * TOP * 16 * B)

        @block.tensor
        def _(pe):
            pe.wait_ge(s_w, WEIGHTS)
            pe.wait_ge(s_const, 3)
            pe.transpose(misc[:, 0:P], wq_nat[:], ident[:]).then_inc(s_wt, 1)
            pe.transpose(misc[:, P:2 * P], wout_nat[:], ident[:]).then_inc(s_wt, 1)
            pe.transpose(misc[0:L, 2 * P:3 * P], qtl_nat[:], ident[:]).then_inc(s_wt, 1)
            pe.wait_ge(s_wc, 3)
            pe.matmul(misc[:, 0:P], wkd[:], qtlT[:], start=True, stop=True).then_inc(s_wt, 1)
            pe.matmul(misc[:, P:2 * P], wvd[:], vup[:].rearrange("l h d -> l (h d)"), start=True, stop=True)\
              .then_inc(s_wt, 1)
            pe.wait_ge(s_wc, 5)

            def score_unit(b, g, k):
                n = exps(b, g, k)
                if k == 0 and g == 0:
                    pe.wait_ge(s_nmd[b.buf], PARTS * 16 * (b.round + 1))
                wait(pe, s_exp, n - 2)
                bank, kk, pr = score[:, k % 2], k % 5, k // 5
                ks, qs = k_stack[b.buf], q_stack[b.buf]
                R = MAX_ROW + PARTS

                def mm(c0, j, h, start):
                    return pe.matmul(bank[:, c0:c0 + T - P * j], ks[0:R, h, P * j:P * j + P], qs[0:R, h, P * j:T],
                                     start=start, stop=True, skip_group_check=True)
                h0 = QUAD * g + 2 * pr
                if kk < 2:
                    last = mm(0, 0, h0 + kk, True)
                elif kk < 4:
                    mm(0, 3, h0 + kk - 2, True)
                    last = mm(P, 1, h0 + kk - 2, False)
                else:
                    mm(0, 2, h0, True)
                    last = mm(2 * P, 2, h0 + 1, False)
                last.then_inc(s_sc, 1)

            def max_bank(b, g, k):
                n = maxes(b, g, k // 2)
                if k == 0 and g == 0:
                    pe.wait_ge(s_stk[b.buf], 6 * 16 * (b.round + 1))
                if k % 2 == 0:
                    wait(pe, s_mx, n - 2)
                bank, kk, pr = maxs[:, (g * MB + k // 2) % 2, k % 2], k % 5, k // 5
                ks, qs = k_stack[b.buf], q_stack[b.buf]

                def mm(c0, i, h, start):
                    pe.matmul(bank[:, c0:c0 + P * (i + 1)], qs[0:MAX_ROW, h, P * i:P * i + P],
                              ks[0:MAX_ROW, h, 0:P * (i + 1)], start=start, stop=False, skip_group_check=True)

                def mask(cols, n):
                    return pe.matmul(cols, ident_bf[:], ahead[:, 0:n], start=False, stop=True, skip_group_check=True)
                h0 = QUAD * g + 2 * pr
                if kk < 2:
                    mm(0, 3, h0 + kk, True)
                    last = mask(bank[:, 3 * P:4 * P], 1)
                elif kk < 4:
                    mm(0, 2, h0 + kk - 2, True)
                    mm(3 * P, 0, h0 + kk - 2, False)
                    last = mask(bank[:, 2 * P:4 * P], 2)
                else:
                    mm(0, 1, h0, True)
                    mm(2 * P, 1, h0 + 1, False)
                    last = mask(bank.rearrange("p (e t) -> p e t", e=2)[:, :, P:2 * P], 2)
                if k % 2:
                    last.then_inc(s_msc, 1)

            def attend(b, g, j):
                if j == 0:
                    pe.wait_ge(s_tri, TRI * (quad(b, g) + 1))
                    wait(pe, s_oc, quad(b, g))
                    if g == 0:
                        pe.wait_ge(s_vc, b.num + 1)
                pt = probs[:, g % 2]
                for q in range(QUAD):
                    v0 = (j * H + QUAD * g + q) * 2 * D
                    pr, e = q // 2, q % 2
                    if j == 0:
                        src = pt[:, 5 * pr + e, :]
                    elif j == 1:
                        src = pt[:, 5 * pr + 2 + e, P:T]
                    elif j == 2:
                        src = pt[:, 5 * pr + 4, 2 * P * e:2 * P * (e + 1)]
                    else:
                        src = pt[:, 5 * pr + 2 + e, 0:P]
                    last = pe.matmul(attn[CT * q:CT * (q + 1), P * j:T], v_aug[:, b.buf, v0:v0 + CT], src,
                                     start=j == 0, stop=j == TT - 1)
                if j == TT - 1:
                    last.then_inc(s_pv, 1)

            def small(b, g, k):
                prev, nxt, far = b.plus(-1), b.plus(1), b.plus(2)
                done = b.plus(-2)
                if (g, k) == (0, 0) and far.exists:
                    pe.wait_ge(s_xin[far.buf], 16 * (far.round + 1))
                    wait(pe, s_vc, far.num)
                    wait(pe, s_nmr, b.num + 1)
                    wait(pe, s_rr, done.num)
                    wait(pe, s_res, done.num + 1)
                    for i in range(TT):
                        last = pe.transpose(misc[:, P * i:P * i + P], x_in[:, far.buf, i, :], ident[:])
                    last.then_inc(s_xt, 1)
                if (g, k) in ((0, 2), (0, 6)) and far.exists:
                    w = int(k == 6)
                    if w == 0:
                        pe.wait_ge(s_xtc, far.num + 1)
                    else:
                        pe.wait_ge(s_rest, 2 * far.num + w)
                    pe.matmul(misc[:], (wqT, wkT)[w][:], xT[:], start=True, stop=True).then_inc(s_proj, 1)
                if (g, k) == (1, 0) and far.exists:
                    pe.wait_ge(s_rest, 2 * far.num + 2)
                    for i in range(TT):
                        last = pe.matmul(misc[:, P * i:P * i + P], xT[:, P * i:P * i + P], wvT[:], start=True, stop=True)
                    last.then_inc(s_v, 1)
                if (g, k) == (1, 3) and done.exists:
                    pe.wait_ge(s_x1, done.num + 1)
                    if far.exists:
                        pe.wait_ge(s_vc, far.num + 1)
                    wait(pe, s_res, done.num + 1)
                    for i in range(TT):
                        last = pe.transpose(misc[:, P * i:P * i + P], image[:, i, 0, 0:E], ident[:])
                    last.then_inc(s_x1t, 1)
                if (g, k) == (1, 5) and done.exists:
                    pe.wait_ge(s_x1tc, done.num + 1)
                    for i in range(TT):
                        last = pe.matmul(misc[:, X * i:X * i + X], x1T[:, P * i:P * i + P], wg[:], start=True, stop=True)
                    last.then_inc(s_lg, 1)
                if (g, k) == (1, 9) and done.exists:
                    pe.wait_ge(s_oh, done.num + 1)
                    n = 0
                    for j in range(TOP):
                        ch = chosen_bf[:, :, j, :]
                        pe.matmul(misc[:, 0:TT * X].rearrange("p (i x) -> p i x", i=TT), before[:], ch, start=j == 0, stop=False,
                                  skip_group_check=True)
                        for s in range(1, TT):
                            pe.matmul(misc[:, s * X:TT * X].rearrange("p (i x) -> p i x", x=X), ones_bf[:], ch[:, 0:TT - s],
                                      start=False, stop=False, skip_group_check=True)
                        for i in range(TT):
                            last = pe.matmul(misc[:, TT * X:TT * X + X], ones_bf[:], ch[:, i], start=False, stop=True,
                                             skip_group_check=True)
                    last.then_inc(s_rk, 1)
                if (g, k) == (3, 2) and nxt.exists:
                    pe.wait_ge(s_rm, nxt.num + 1)
                    if far.exists:
                        pe.wait_ge(s_vc, far.num + 1)
                    wait(pe, s_rr, done.num + 1)
                    wait_apart(pe, s_res, prev.num, s_passed_pe)
                    pe.transpose(misc[0:H * TT, 0:P], row_max[:].rearrange("p h i -> p (h i)"), ident[:]).then_inc(s_nmt, 1)
                if (g, k) == (3, 7) and prev.exists:
                    if nxt.exists:
                        pe.wait_ge(s_nmr, nxt.num + 1)
                    wait(pe, s_rr, done.num + 1)
                    wait(pe, s_res, prev.num)
                    pe.wait_ge(s_ht, prev.num + 1)
                    for i in range(TT):
                        last = pe.matmul(misc[:, P * i:P * i + P], headsT[:, P * i:P * i + P], woutT[:], start=True, stop=True)
                    last.then_inc(s_op, 1)

            ATTEND_AT = (4, 5, 7, 9)

            def step(b):
                for g in range(QUADS):
                    mb, mg = (b.plus(1), g + 1) if g + 1 < QUADS else (b.plus(2), 0)
                    pb, pg = (b, g - 1) if g else (b.plus(-1), QUADS - 1)
                    for k in range(EB):
                        if b.exists:
                            score_unit(b, g, k)
                        small(b, g, k)
                        if mb.exists:
                            max_bank(mb, mg, k)
                        if pb.exists and k in ATTEND_AT:
                            attend(pb, pg, ATTEND_AT.index(k))

            over_batches(pe, B, step)

        @block.scalar
        def _(act):
            act.preload_act_table_set("natural_log_exp_and_others")

            def step(b):
                prev, nxt, far, done = b.plus(-1), b.plus(1), b.plus(2), b.plus(-2)
                for g in range(QUADS):
                    ob, og = (b, g - 2) if g >= 2 else (b.plus(-1), g + QUADS - 2)
                    for k in range(EB):
                        if b.exists:
                            if k == 0:
                                wait(act, s_pv, quad(b, g) - 1)
                            act.wait_ge(s_sc, exps(b, g, k))
                            act.activation(probs[:, g % 2, k, :], score[:, k % 2], ACT.Exp).then_inc(s_exp, 1)
                        if (g, k) == (0, 0) and far.exists:
                            act.wait_ge(s_xt, far.num + 1)
                            wait(act, s_v, far.num)
                            act.activation(xT[:], misc[:], ACT.Copy).then_inc(s_xtc, 1)
                        if (g, k) == (1, 0) and far.exists:
                            act.wait_ge(s_v, far.num + 1)
                            act.wait_ge(s_vones, far.buf + 1)
                            wait(act, s_pv, quad(far.plus(-STACK), QUADS - 1) + 1)
                            v_rows = v_aug[:, far.buf, 0:TT * H * 2 * D].rearrange("p (n d) -> p n d", d=2 * D)
                            act.activation(v_rows[:, :, 0:D], misc[:].rearrange("p (n d) -> p n d", d=D), ACT.Copy)\
                               .then_inc(s_vc, 1)
                        if (g, k) in ((0, 5), (0, 9)) and far.exists:
                            w = int(k == 9)
                            act.wait_ge(s_rest, 2 * far.num + w + 1)
                            act.activation(qk_parts[w][:, 1, :], qk_rest[w][:], ACT.Copy).then_inc(s_mid, 1)
                        if (g, k) in ((0, 2), (0, 6)) and far.exists:
                            w = int(k == 6)
                            act.wait_ge(s_proj, 2 * far.num + w + 1)
                            before = far.plus(-1)
                            wait(act, s_pst[w][before.buf], PARTS * 16 * (before.round + 1))
                            act.activation(qk_parts[w][:, 0, :], misc[:], ACT.Copy).then_inc(s_hi, 1)
                        if ob.exists and k == 1 and og % 2 == 0:
                            act.wait_ge(s_pv, quad(ob, og) + 1)
                            if og == 0:
                                before = ob.plus(-1)
                                wait(act, s_hd[before.buf], QUAD * 16 * (before.round + 1))
                            act.activation(heads_out[:, og], attn[:], ACT.Copy).then_inc(s_oc, 1)
                        if (g, k) == (3, 2) and nxt.exists:
                            act.wait_ge(s_nmt, nxt.num + 1)
                            wait(act, s_nmd[b.buf], PARTS * 16 * (b.round + 1))
                            act.activation(max_parts[:, 0, :], misc[0:H * TT, 0:P], ACT.Copy, scale=-1.0).then_inc(s_nm0, 1)
                        if (g, k) == (1, 3) and done.exists:
                            act.wait_ge(s_x1t, done.num + 1)
                            act.activation(x1T[:], misc[:], ACT.Copy).then_inc(s_x1tc, 1)
                        if (g, k) == (1, 8) and done.exists:
                            act.wait_ge(s_gap, done.num + 1)
                            act.activation(odds[:], gap[:], ACT.Exp).then_inc(s_odds, 1)
                        if (g, k) == (0, 3) and done.exists:
                            act.wait_ge(s_st, 2 * (done.num + 1))
                            act.activation(log_var[:], mean_var[:, :, 1], ACT.Ln, bias=eps_col[:]).then_inc(s_ln, 1)
                            act.wait_ge(s_ln, done.num + 1)
                            act.activation(rstd[:], log_var[:], ACT.Exp, scale=-0.5).then_inc(s_rs, 1)

            act.wait_ge(s_const, 6)
            over_batches(act, B, step)

        @block.vector
        def _(dve):
            for i in range(STACK):
                dve.memset(v_aug[:, i], 1.0).then_inc(s_vones, 1)
            for n, (dst, src, scale) in enumerate([
                (wqT[:], misc[:, 0:P], SC), (woutT[:], misc[:, P:2 * P], 1.0), (qtlT[:], misc[0:L, 2 * P:3 * P], 1.0),
                (wkT[:], misc[:, 0:P], 1.0), (wvT[:], misc[:, P:2 * P], 1.0),
            ]):
                dve.wait_ge(s_wt, 3 if n < 3 else 5)
                dve.tensor_scalar_mul(dst, src, scale).then_inc(s_wc, 1)

            dve.wait_ge(s_const, 12)
            dve.tensor_copy(iota_x[:], iota_i[:]).then_inc(s_ch, 1)
            dve.tensor_copy(dest[:].rearrange("p i j -> p (i j)"), dest_i[:]).then_inc(s_ch, 1)
            dve.wait_ge(s_ch, 2)
            dve.tensor_scalar_mul(region0[:], iota_x[:], float(REGION)).then_inc(s_ch, 1)
            dve.tensor_scalar_mul(base[:], iota_x[:], float(REGION)).then_inc(s_ch, 1)
            dve.wait_ge(s_const, 16)
            dve.memset(lead[:, X:X + 1], float(SPARE)).then_inc(s_plan0, 1)
            dve.tensor_copy(iota_j[:], iota_ji[:]).then_inc(s_plan0, 1)
            dve.wait_ge(s_plan0, 2)
            dve.tensor_scalar_mul(job_sf[:], iota_j[:], float(P)).then_inc(s_plan0, 1)
            dve.wait_ge(s_plan0, 3)
            CHOICE, PLACE = 4, 8

            def choose(b):
                n = 4 + CHOICE * b.num
                dve.wait_ge(s_lg, b.num + 1)
                dve.tensor_copy(logits[:].rearrange("p i x -> p (i x)"), misc[:, 0:TT * X]).then_inc(s_ch, 1)
                wait_apart(dve, s_ch, n + 1, s_passed_dve)
                for i in range(TT):
                    last = dve.max(top[:, i], logits[:, i])
                last.then_inc(s_ch, 1)
                dve.wait_ge(s_ch, n + 2)
                dve.tensor_tensor(gap[:], top[:, :, 1], top[:, :, 0], ALU.subtract).then_inc(s_gap, 1)
                for i in range(TT):
                    last = dve.max_index(top_at[:, i], top[:, i], logits[:, i])
                last.then_inc(s_ch, 1)
                dve.wait_ge(s_ch, n + 3)
                dve.tensor_copy(top_f[:], top_at[:, :, 0:TOP]).then_inc(s_ch, 1)
                dve.wait_ge(s_ch, n + 4)
                dve.tensor_tensor(chosen_bf[:].rearrange("p i j x -> p (i j) x"),
                                  iota_x[:].rearrange("p (o x) -> p o x", o=1).to_broadcast([P, TT * TOP, X]),
                                  top_f[:].rearrange("p i (j o) -> p (i j) o", o=1).to_broadcast([P, TT * TOP, X]),
                                  ALU.is_equal).then_inc(s_oh, 1)

            def rank(b):
                n = PLACE * b.num
                dve.wait_ge(s_rk, b.num + 1)
                dve.tensor_tensor(row_of[:], misc[:, 0:TT * X].rearrange("p (i x) -> p i x", x=X),
                                  base[:].rearrange("p (o x) -> p o x", o=1).to_broadcast([P, TT, X]), ALU.add).then_inc(s_ro, 1)
                dve.wait_ge(s_ro, n + 1)
                dve.tensor_tensor(base[:], base[:], misc[:, TT * X:TT * X + X], ALU.add).then_inc(s_rr, 1)

            def place(b):
                n = PLACE * b.num
                for j in range(TOP):
                    last = dve.tensor_tensor(picked[:, :, j], row_of[:], chosen_bf[:, :, j], ALU.mult)
                last.then_inc(s_ro, 1)
                dve.wait_ge(s_ro, n + 2)
                dve.tensor_reduce(row_f[:].rearrange("p i j -> p (i j)"), picked[:].rearrange("p i j x -> p (i j) x"),
                                  AX.X, ALU.add).then_inc(s_ro, 1)
                dve.wait_ge(s_odds, b.num + 1)
                dve.tensor_scalar_add(odds1[:], odds[:], 1.0).then_inc(s_ro, 1)
                dve.wait_ge(s_ro, n + 4)
                dve.reciprocal(image[:, :, 0, E], odds1[:]).then_inc(s_ro, 1)
                dve.wait_ge(s_ro, n + 5)
                dve.tensor_tensor(image[:, :, 1, E], odds[:], image[:, :, 0, E], ALU.mult).then_inc(s_ro, 1)
                dve.tensor_copy(image[:, :, :, E + 1], dest[:]).then_inc(s_ro, 1)
                dve.wait_ge(s_ro, n + 7)
                dve.tensor_scalar_add(dest[:], dest[:], float(T)).then_inc(s_ro, 1)
                dve.wait_ge(s_ro, n + 8)
                dve.tensor_copy(row_i[:], row_f[:]).then_inc(s_rows, 1)

            def max_unit(b, g, m):
                dve.wait_ge(s_msc, maxes(b, g, m))
                flat = part_max[:].rearrange("p a k i -> p (a k i)")
                first = (g * MB + m) * 8
                if m == 0 and g == 0:
                    wait(dve, s_rm, b.num)
                dve.tensor_reduce(flat[:, first:first + 8],
                                  maxs[:, (g * MB + m) % 2].rearrange("p c (i t) -> p (c i) t", t=P), AX.X, ALU.max)\
                   .then_inc(s_mx, 1)

            def step(b):
                prev, nxt, far, done = b.plus(-1), b.plus(1), b.plus(2), b.plus(-2)
                for g in range(QUADS):
                    mb, mg = (b.plus(1), g + 1) if g + 1 < QUADS else (b.plus(2), 0)
                    ob, og = (b, g - 2) if g >= 2 else (b.plus(-1), g + QUADS - 2)
                    for m in range(MB):
                        if mb.exists:
                            max_unit(mb, mg, m)
                        if ob.exists and m == 0 and og % 2 == 1:
                            dve.wait_ge(s_pv, quad(ob, og) + 1)
                            dve.tensor_copy(heads_out[:, og], attn[:]).then_inc(s_oc, 1)
                        if (g, m) in ((0, 1), (0, 3)) and far.exists:
                            w = int(m == 3)
                            dve.wait_ge(s_hi, 2 * far.num + w + 1)
                            dve.tensor_tensor(qk_rest[w][:], misc[:], qk_parts[w][:, 0, :], ALU.subtract).then_inc(s_rest, 1)
                        if (g, m) == (1, 2) and done.exists:
                            choose(done)
                        if (g, m) == (2, 0) and done.exists:
                            rank(done)
                        if (g, m) == (2, 1) and done.exists:
                            place(done)
                        if (g, m) == ((1, 4) if b.exists else (2, 2)) and prev.exists:
                            dve.wait_ge(s_nd[prev.buf], 2 * 16 * (prev.round + 1))
                            dve.reciprocal(rden[:], denom[:]).then_inc(s_rd, 1)
                        if (g, m) == (0, 2) and done.exists:
                            dve.wait_ge(s_rs, done.num + 1)
                            wait(dve, s_out, 16 * done.num)
                            wait(dve, s_sct, TT * TOP * 16 * done.num)
                            for i in range(TT):
                                last = dve.tensor_scalar(image[:, i, 0, 0:E], x_res[:, done.buf, i], mean_var[:, i, 0:1],
                                                         rstd[:, i:i + 1], ALU.subtract, ALU.mult)
                            last.then_inc(s_x1, 1)
                        if (g, m) == (3, 2) and nxt.exists:
                            dve.wait_ge(s_nm0, nxt.num + 1)
                            dve.scalar_tensor_tensor(out=max_rest[:], in0=misc[0:H * TT, 0:P], scalar=-1.0,
                                                     in1=max_parts[:, 0, :], op0=ALU.mult, op1=ALU.subtract).then_inc(s_nmr, 1)
                            dve.wait_ge(s_nmr, nxt.num + 1)
                            dve.tensor_copy(max_parts[:, 1, :], max_rest[:]).then_inc(s_nm1, 1)
                            dve.wait_ge(s_nm1, nxt.num + 1)
                            dve.tensor_tensor(max_parts[:, 2, :], max_rest[:], max_parts[:, 1, :], ALU.subtract)\
                               .then_inc(s_nmp, 1)
                        if (g, m) == (3, 3) and prev.exists:
                            dve.wait_ge(s_op, prev.num + 1)
                            dve.wait_ge(s_xres[prev.buf], 16 * (prev.round + 1))
                            resid = x_res[:, prev.buf]
                            dve.tensor_tensor(resid.rearrange("p i e -> p (i e)"), misc[:],
                                              resid.rearrange("p i e -> p (i e)"), ALU.add).then_inc(s_res, 1)
                        if (g, m) == (3, 4) and prev.exists:
                            dve.wait_ge(s_res, prev.num + 1)
                            for i in range(TT):
                                last = dve.bn_stats(stats[:, i], x_res[:, prev.buf, i])
                            last.then_inc(s_st, 1)
                            wait_apart(dve, s_st, 2 * prev.num + 1, s_passed_dve)
                            for i in range(TT):
                                last = dve.bn_aggr(mean_var[:, i], stats[:, i])
                            last.then_inc(s_st, 1)
                    if g == 2 and nxt.exists:
                        pm = part_max[:]
                        dve.wait_ge(s_mx, maxes(nxt, QUADS - 1, MB - 1))
                        wait(dve, s_nmt, nxt.num)
                        rm = row_max[:].rearrange("p (a e) i -> p a e i", e=2)
                        dve.tensor_reduce(rm[:, :, :, 3], pm[:, :, 0:2, :], AX.X, ALU.max)
                        dve.tensor_reduce(rm[:, :, :, 2], pm[:, :, 2:4, 0:3], AX.X, ALU.max)
                        dve.tensor_reduce(rm[:, :, :, 1], pm[:, :, 4, :].rearrange("p a (e i) -> p a e i", e=2), AX.X, ALU.max)
                        dve.tensor_copy(rm[:, :, :, 0], pm[:, :, 2:4, 3]).then_inc(s_rm, 1)

            over_batches(dve, B, step)

            done = [0]

            def link(ins):
                done[0] += 1
                ins.then_inc(s_pl, 1)
                dve.wait_ge(s_pl, done[0])

            def along(ap):
                return ap.rearrange("p (o x) -> p o x", o=1).to_broadcast([1, JOBS, X])

            def across(ap):
                return ap.rearrange("p (j o) -> p j o", o=1).to_broadcast([1, JOBS, X])

            dve.wait_ge(s_rr, B)
            dve.tensor_copy(pad_i[:], base[:]).then_inc(s_padi, 1)
            link(dve.scalar_tensor_tensor(out=rows_n[:], in0=base[:], scalar=float(P - 1), in1=region0[:],
                                          op0=ALU.add, op1=ALU.subtract))
            link(dve.tensor_copy(tiles_i[:], rows_n[:]))
            link(dve.tensor_single_scalar(tiles_i[:], tiles_i[:], P.bit_length() - 1, ALU.arith_shift_right))
            link(dve.tensor_copy(tiles[:], tiles_i[:]))
            link(dve.tensor_tensor_scan(tile_end[:], ones_x[:], tiles[:], 0.0, ALU.mult, ALU.add))
            link(dve.tensor_tensor(tile_start[:], tile_end[:], tiles[:], ALU.subtract))
            dve.tensor_tensor(past_end, across(iota_j[0:1, :]), along(tile_end[0:1, :]), ALU.is_ge).then_inc(s_past, 1)
            link(dve.scalar_tensor_tensor(out=lead[:, 0:X], in0=tile_start[:], scalar=-float(P), in1=region0[:],
                                          op0=ALU.mult, op1=ALU.add))
            link(dve.tensor_tensor(lead_step[:], lead[:, 1:X + 1], lead[:, 0:X], ALU.subtract))
            dve.wait_ge(s_past, 1)
            link(dve.tensor_tensor(steps_past, past_end, along(lead_step[0:1, :]), ALU.mult))
            dve.tensor_reduce(job_xf[:], past_end, AX.X, ALU.add).then_inc(s_past, 1)
            link(dve.tensor_reduce(job_rf[:], steps_past, AX.X, ALU.add))
            link(dve.scalar_tensor_tensor(out=job_rf[:], in0=job_rf[:], scalar=lead[0:1, 0:1], in1=job_sf[:],
                                          op0=ALU.add, op1=ALU.add))
            dve.wait_ge(s_past, 2)
            dve.tensor_scalar_min(job_xf[:], job_xf[:], float(X - 1)).then_inc(s_past, 1)
            link(dve.tensor_scalar_min(job_rf[:], job_rf[:], float(SPARE)))
            dve.wait_ge(s_past, 3)
            dve.tensor_copy(job_x[:], job_xf[:]).then_inc(s_pl, 1)
            dve.tensor_copy(job_row[:], job_rf[:]).then_inc(s_pl, 1)

    experts(nc, B, T, E, X, F, ROW, SPARE, JOBS, xs_dram, y_dram, x1_dram, out,
            job_x, job_row, w13, w2s, ident, eps_col)
    keep.close()


def experts(nc, B, T, E, X, F, ROW, SPARE, JOBS, xs_dram, y_dram, x1_dram, out,
            job_x, job_row, w13, w2s, ident, eps_col):
    TT = T // P
    TOP = 2
    FC = F // P
    TOKENS = B * T
    XR = 8
    YR = 8
    TR = 4
    UNROLL = 16
    AHEAD = 2
    ctx = ExitStack()
    with ctx:
        def sb(name, shape, dt=FP32):
            return ctx.enter_context(nc.sbuf_tensor(name, shape, dt))

        def ps(name, shape, dt=FP32):
            return ctx.enter_context(nc.psum_tensor(name, shape, dt))

        def sem(name):
            return ctx.enter_context(nc.semaphore(name))

        def sems(name, n):
            return [sem(f"{name}{i}") for i in range(n)]

        rows = sb("rows", [P, XR, ROW])
        rowsT = sb("rowsT", [E, TR, P])
        gate = sb("gate", [P, 2, F])
        hid = sb("hid", [P, 2, F])
        hidT = sb("hidT", [P, 2, FC, P])
        res = sb("res", [P, YR, E])
        res_to = sb("res_to", [P, YR], UINT32)
        RB = 4
        NB = 8
        xa = sb("xa", [P, B, TT, E])
        ya = sb("ya", [P, NB, TOP, TT, E])
        yy = sb("yy", [P, RB, TT, E])
        tot = sb("tot", [P, RB, TT, E])
        stats = sb("stats2", [P, TT, 6])
        mean_var = sb("mean_var2", [P, RB, TT, 2])
        log_var = sb("log_var2", [P, RB, TT])
        rstd = sb("rstd2", [P, RB, TT])
        shift = sb("shift", [P, RB, TT])
        fin = sb("fin", [P, RB, TT, E])

        psX = ps("psX", [P, 2, T])
        psH = ps("psH", [P, 2, T])
        psT = ps("psT", [P, 2, T])
        psY = ps("psY", [P, 2, T])

        s_passed_pool = sem("pool_passed2")
        s_x = sems("rows_loaded", XR)
        s_xt = sem("rows_transposed")
        s_xc = sem("rowsT_copied")
        s_h = sem("hidden_ready")
        s_g = sem("gate_made")
        s_m = sem("hidden_made")
        s_ht = sem("hidden_transposed")
        s_hc = sem("hiddenT_copied")
        s_y = sem("result_ready")
        s_to = sem("destination_made")
        s_yc = sem("result_scaled")
        s_sc = sems("result_scattered", YR)
        s_l = sems("results_loaded", NB)
        s_xa = sem("x1_loaded")
        s_a1 = sem("results_added")
        s_a2 = sem("total_made")
        s_st = sem("stats_made2")
        s_mv = sem("mean_var_made2")
        s_lg = sem("log_made2")
        s_rs = sem("rstd_made2")
        s_sh = sem("shift_made")
        s_f = sem("final_made")
        s_o = sems("out_stored", RB)

        x_v = x1_dram.rearrange("(b i p) e -> b p i e", p=P, i=TT)
        y_v = y_dram.rearrange("(j b i p) e -> j b p i e", p=P, i=TT, j=TOP)
        o_v = out.rearrange("b (i p) e -> b p i e", p=P)

        def over_jobs(eng, step, lead, lag):
            lo, hi = 2 * XR, JOBS - lag
            turns = (hi - lo - lead) // UNROLL
            for n in range(-lead, lo):
                step(n, n % XR)
            with eng.Fori(0, turns) as i:
                for t in range(UNROLL):
                    step(i * UNROLL + lo + t, t)
            for n in range(lo + turns * UNROLL, JOBS + lag):
                step(n, n % XR)

        def is_job(n):
            return not isinstance(n, int) or 0 <= n < JOBS

        block = ctx.enter_context(nc.Block())

        @block.sync
        def _(sp):
            def step(n, t):
                u = t % XR
                if is_job(n):
                    wait(sp, s_yc, n - XR + 1)
                    row = sp.value_load(job_row[0:1, bass.ds(n, 1)], min_val=0, max_val=SPARE)
                    sp.dma_start(rows[:, u, :], xs_dram[bass.ds(row, P), :]).then_inc(s_x[u], 16)
                if isinstance(n, int) and AHEAD < n < 2 * XR:
                    for b in range(n - AHEAD - 1, B, 2 * XR - AHEAD - 1):
                        sp.dma_start(xa[:, b], x_v[b]).then_inc(s_xa, 16)

            over_jobs(sp, step, 0, 0)
            for u in range(YR):
                sp.wait_ge(s_sc[u], 16 * len(range(u, JOBS, YR)))
            for b in range(B):
                wait(sp, s_a1, b - NB + 1)
                for j in range(TOP):
                    sp.dma_start(ya[:, b % NB, j], y_v[j, b]).then_inc(s_l[b % NB], 16)
            for b in range(B):
                sp.wait_ge(s_f, b + 1)
                sp.dma_start(o_v[b], fin[:, b % RB]).then_inc(s_o[b % RB], 16)
            for u in range(RB):
                sp.wait_ge(s_o[u], 16 * len(range(u, B, RB)))

        @block.gpsimd
        def _(pool):
            def step(n, t):
                u = t % YR
                if is_job(n):
                    wait_apart(pool, s_yc, n + 1, s_passed_pool)
                    wait_apart(pool, s_to, n + 1, s_passed_pool)
                    pool.indirect_dma_start(out=y_dram, out_offset=bass.IndirectOffsetOnAxis(ap=res_to[:, u:u + 1], axis=0),
                                            in_=res[:, u, :], in_offset=None, bounds_check=TOP * TOKENS - 1,
                                            oob_is_err=False).then_inc(s_sc[u], 16)
            over_jobs(pool, step, 0, 0)

            for b in range(B):
                pool.wait_ge(s_l[b % NB], TOP * 16 * (b // NB + 1))
                wait(pool, s_a2, b - RB + 1)
                pool.tensor_tensor(yy[:, b % RB], ya[:, b % NB, 0], ya[:, b % NB, 1], ALU.add).then_inc(s_a1, 1)

        @block.tensor
        def _(pe):
            loaded = {}

            def expert_of(n, t, k):
                if not isinstance(n, int) and t == 0 and k == 0:
                    loaded.clear()
                key = n + k if isinstance(n, int) else ("turn", t + k)
                if key not in loaded:
                    loaded[key] = pe.value_load(job_x[0:1, bass.ds(n + k, 1)], min_val=0, max_val=X - 1)
                return loaded[key]

            def step(n, t):
                u, v = t % XR, t % 2
                ahead, back, back2 = n + AHEAD, n - 1, n - 2
                if is_job(ahead):
                    a = (u + AHEAD) % XR
                    pe.wait_ge(s_x[a], rounds(ahead, a))
                    wait(pe, s_xc, ahead - 1)
                    pe.transpose(psX[:, a % 2, 0:P], rows[:, a, 0:E], ident[:]).then_inc(s_xt, 1)
                if is_job(n):
                    x = expert_of(n, t, 0)
                    pe.wait_ge(s_xc, n + 1)
                    wait(pe, s_m, n - 1)
                    pe.matmul(psH[:, v, :], rowsT[:, u % TR, :], w13[:, bass.ds(x, 1), :].rearrange("p o f -> p (o f)"),
                              start=True, stop=True).then_inc(s_h, 1)
                load_next = is_job(n + 1) and (isinstance(n, int) or t + 1 < UNROLL)
                two_needed = not isinstance(n, int) and t < 2
                if is_job(back2):
                    x2 = expert_of(n, t, -2)
                if load_next and not two_needed:
                    expert_of(n, t, 1)
                if is_job(back):
                    pe.wait_ge(s_m, back + 1)
                    wait(pe, s_hc, back - 1)
                    for c in range(FC):
                        last = pe.transpose(psT[:, 1 - v, P * c:P * c + P], hid[:, 1 - v, P * c:P * c + P], ident[:])
                    last.then_inc(s_ht, 1)
                if load_next and two_needed:
                    expert_of(n, t, 1)
                if is_job(back2):
                    pe.wait_ge(s_hc, back2 + 1)
                    wait(pe, s_yc, back2 - 1)
                    for c in range(FC):
                        last = pe.matmul(psY[:, v, 0:E], hidT[:, v, c, :], w2s[:, bass.ds(x2, 1), c, :].rearrange("p o e -> p (o e)"),
                                         start=c == 0, stop=c == FC - 1)
                    last.then_inc(s_y, 1)

            def rounds(n, u):
                if isinstance(n, int):
                    return 16 * (n // XR + 1)
                return (n - (u % XR)) * (16 // XR) + 16
            over_jobs(pe, step, AHEAD, 2)

        @block.scalar
        def _(act):
            act.preload_act_table(ACT.Silu)

            def step(n, t):
                u, v = t % XR, t % 2
                ahead, back2 = n + AHEAD, n - 2
                if is_job(ahead):
                    a = (u + AHEAD) % XR
                    act.wait_ge(s_xt, ahead + 1)
                    wait(act, s_h, ahead - TR + 1)
                    act.activation(rowsT[:, a % TR, :], psX[:, a % 2, 0:P], ACT.Copy).then_inc(s_xc, 1)
                if is_job(n):
                    act.wait_ge(s_h, n + 1)
                    wait(act, s_m, n - 1)
                    act.activation(gate[:, v, :], psH[:, v, 0:F], ACT.Silu).then_inc(s_g, 1)
                if is_job(back2):
                    w = (u - 2) % YR
                    act.wait_ge(s_y, back2 + 1)
                    if not isinstance(back2, int) or back2 >= YR:
                        act.wait_ge(s_sc[w], rounds(back2, w) - 16)
                    act.activation(res[:, w, :], psY[:, v, 0:E], ACT.Copy, scale=rows[:, w, E:E + 1]).then_inc(s_yc, 1)

            def rounds(n, u):
                if isinstance(n, int):
                    return 16 * (n // YR + 1)
                return (n - (u % YR)) * (16 // YR) + 16
            over_jobs(act, step, AHEAD, 2)
            act.preload_act_table_set("natural_log_exp_and_others")
            def scale(b):
                act.wait_ge(s_mv, b + 1)
                act.activation(log_var[:, b % RB], mean_var[:, b % RB, :, 1], ACT.Ln, bias=eps_col[:]).then_inc(s_lg, 1)
                act.wait_ge(s_lg, b + 1)
                act.activation(rstd[:, b % RB], log_var[:, b % RB], ACT.Exp, scale=-0.5).then_inc(s_rs, 1)

            def normalize(b):
                act.wait_ge(s_sh, b + 1)
                if b >= RB:
                    act.wait_ge(s_o[b % RB], 16 * (b // RB))
                for i in range(TT):
                    last = act.activation(fin[:, b % RB, i], tot[:, b % RB, i], ACT.Identity, bias=shift[:, b % RB, i:i + 1],
                                          scale=rstd[:, b % RB, i:i + 1])
                last.then_inc(s_f, 1)

            for b in range(B):
                scale(b)
                if b:
                    normalize(b - 1)
            normalize(B - 1)
        @block.vector
        def _(dve):
            def step(n, t):
                u, v = t % XR, t % 2
                back = n - 1
                if is_job(n):
                    w = u % YR
                    if not isinstance(n, int) or n >= YR:
                        dve.wait_ge(s_sc[w], rounds(n, w) - 16)
                    dve.wait_ge(s_h, n + 1)
                    dve.tensor_copy(res_to[:, w:w + 1], rows[:, u, E + 1:E + 2]).then_inc(s_to, 1)
                    dve.wait_ge(s_g, n + 1)
                    wait(dve, s_ht, n - 1)
                    dve.tensor_tensor(hid[:, v, :], gate[:, v, :], psH[:, v, F:2 * F], ALU.mult).then_inc(s_m, 1)
                if is_job(back):
                    dve.wait_ge(s_ht, back + 1)
                    wait(dve, s_y, back - 1)
                    dve.tensor_copy(hidT[:, 1 - v].rearrange("p c t -> p (c t)"), psT[:, 1 - v, 0:F]).then_inc(s_hc, 1)

            def rounds(n, u):
                if isinstance(n, int):
                    return 16 * (n // YR + 1)
                return (n - (u % YR)) * (16 // YR) + 16
            over_jobs(dve, step, 0, 1)

            def total(b):
                dve.wait_ge(s_a1, b + 1)
                wait(dve, s_f, b - RB + 1)
                dve.tensor_tensor(tot[:, b % RB], xa[:, b], yy[:, b % RB], ALU.add).then_inc(s_a2, 1)
                dve.wait_ge(s_a2, b + 1)
                for i in range(TT):
                    last = dve.bn_stats(stats[:, i], tot[:, b % RB, i])
                last.then_inc(s_st, 1)
                dve.wait_ge(s_st, b + 1)
                for i in range(TT):
                    last = dve.bn_aggr(mean_var[:, b % RB, i], stats[:, i])
                last.then_inc(s_mv, 1)

            def shift_of(b):
                dve.wait_ge(s_rs, b + 1)
                dve.scalar_tensor_tensor(out=shift[:, b % RB], in0=mean_var[:, b % RB, :, 0], scalar=-1.0, in1=rstd[:, b % RB],
                                         op0=ALU.mult, op1=ALU.mult).then_inc(s_sh, 1)

            dve.wait_ge(s_xa, 16 * B)
            for b in range(B):
                total(b)
                if b:
                    shift_of(b - 1)
            shift_of(B - 1)


_INS = ["L0_attn_hidden_states", "L0_attn_Wq", "L0_attn_Wk_down", "L0_attn_Wv_down", "L0_attn_q_to_latent",
        "L0_attn_v_up", "L0_attn_Wout", "L0_ffn_w_gate", "L0_ffn_w1", "L0_ffn_w3", "L0_ffn_w2"]


def kernel(**inputs):
    import numpy as _np
    import concourse.bacc as _bacc
    from concourse.bass_utils import run_bass_kernel_spmd as _run

    nc = _bacc.Bacc("TRN2", target_bir_lowering=False, num_devices=1)
    arrays, args = {}, []
    for name in _INS:
        a = _np.ascontiguousarray(inputs[name])
        arrays[f"in_{name}_dram"] = a
        args.append(nc.dram_tensor(f"in_{name}_dram", a.shape, mybir.dt.from_np(a.dtype), kind="ExternalInput").ap())
    shape = inputs[_INS[0]].shape
    out = nc.dram_tensor("out_dram", shape, FP32, kind="ExternalOutput").ap()
    build(nc, *args, out)
    r = _run(nc, [arrays], core_ids=[0])
    return r.results[0]["out_dram"]
```
